# Optimizing a Trainium2 kernel written in Bass

```python
import numpy as np
import jax
import jax.numpy as jnp

def _softmax(x, axis=-1):
    return jax.nn.softmax(x, axis=axis)

def _gelu(x):
    return jax.nn.gelu(x, approximate=True)

def _silu(x):
    return jax.nn.silu(x)

def _sigmoid(x):
    return jax.nn.sigmoid(x)

def _layernorm(x, axis=-1, eps=1e-05):
    m = jnp.mean(x, axis=axis, keepdims=True)
    v = jnp.var(x, axis=axis, keepdims=True)
    return (x - m) / jnp.sqrt(v + eps)

def _scatter_add(tgt, idx, src, axis=0):
    return tgt.at[idx].add(src)

def _segment_sum(src, seg, n):
    return jax.ops.segment_sum(src, seg, n)
kernel_name = 'mk_gnn_resnorm_d1_gnn_r8_15c3ff'

def setup_inputs(seed: int=0):
    np.random.seed(seed)
    _w = jnp.asarray

    def _rec_inputs():
        import jax
        import jax.numpy as jnp
        _gk = jax.random.key(seed)
        x = -0.0001126 + 1 * jax.random.normal(jax.random.fold_in(_gk, 1), (1250, 768), jnp.float32)
        _s = jax.random.randint(jax.random.fold_in(_gk, 2), (20000,), 0, 1250, jnp.int32)
        _d = jax.random.randint(jax.random.fold_in(_gk, 3), (20000,), 0, 1250, jnp.int32)
        _loop = jnp.arange(1250, dtype=jnp.int32)
        src = jnp.concatenate([_s, _d, _loop])
        dst = jnp.concatenate([_d, _s, _loop])
        _o = jnp.argsort(dst, stable=True)
        src = src[_o]
        dst = dst[_o]
        edge_weight1 = -0.00472126 + 0.997171 * jax.random.normal(jax.random.fold_in(_gk, 13), (41250, 1), jnp.float32)
        return (x, src, dst, edge_weight1)
    x, src, dst, edge_weight1 = _rec_inputs()

    def _L0_gnn_setup():
        import jax, jax.numpy as jnp
        import numpy as np
        N, E, D, H, C = (1250, 12500, 768, 4, 192)
        NEG_SLOPE = 0.2

        def gat_conv(x, src, dst, W, a_src, a_dst, b):
            h = (x @ W).reshape(N, H, C)
            as_n = (h * a_src).sum(-1)
            ad_n = (h * a_dst).sum(-1)
            e = jax.nn.leaky_relu(as_n[src] + ad_n[dst], NEG_SLOPE)
            m = jax.ops.segment_max(e, dst, num_segments=N)
            p = jnp.exp(e - m[dst])
            s = jax.ops.segment_sum(p, dst, num_segments=N)
            alpha = p / (s[dst] + 1e-16)
            out = jax.ops.segment_sum(alpha[:, :, None] * h[src], dst, num_segments=N)
            return out.reshape(N, H * C) + b
        key = jax.random.key(seed)
        ks = jax.random.split(key, 16)
        w = lambda k, shape: jax.random.normal(k, shape, dtype=jnp.float32) * 0.02
        inp = {}
        inp['x'] = jax.random.normal(ks[0], (N, D), dtype=jnp.float32)
        inp['edge_index'] = jax.random.randint(ks[1], (2, E), 0, N, dtype=jnp.int32)
        inp['batch'] = jnp.zeros((N,), dtype=jnp.int32)
        inp['edge_attr'] = jax.random.normal(ks[2], (E, 1), dtype=jnp.float32)
        inp['W_ah'] = w(ks[3], (D, D))
        inp['b_ah'] = jnp.zeros((D,), jnp.float32)
        for i in range(3):
            inp[f'W{i}'] = w(ks[4 + 3 * i], (D, H * C))
            inp[f'a_src{i}'] = w(ks[5 + 3 * i], (H, C))
            inp[f'a_dst{i}'] = w(ks[6 + 3 * i], (H, C))
            inp[f'b{i}'] = jnp.zeros((H * C,), jnp.float32)
        inp['W_out'] = w(ks[13], (3 * D, D))
        inp['b_out'] = jnp.zeros((D,), jnp.float32)
        return inp
    _L0_gnn_all = _L0_gnn_setup()
    _L0_gnn_in = {k: v for k, v in _L0_gnn_all.items() if k in ('W_ah', 'b_ah', 'W0', 'a_src0', 'a_dst0', 'b0', 'W1', 'a_src1', 'a_dst1', 'b1', 'W2', 'a_src2', 'a_dst2', 'b2', 'W_out', 'b_out')}
    del _L0_gnn_all
    return {'x': x, 'src': src, 'dst': dst, 'edge_weight1': edge_weight1, 'L0_gnn_W_ah': _L0_gnn_in['W_ah'], 'L0_gnn_b_ah': _L0_gnn_in['b_ah'], 'L0_gnn_W0': _L0_gnn_in['W0'], 'L0_gnn_a_src0': _L0_gnn_in['a_src0'], 'L0_gnn_a_dst0': _L0_gnn_in['a_dst0'], 'L0_gnn_b0': _L0_gnn_in['b0'], 'L0_gnn_W1': _L0_gnn_in['W1'], 'L0_gnn_a_src1': _L0_gnn_in['a_src1'], 'L0_gnn_a_dst1': _L0_gnn_in['a_dst1'], 'L0_gnn_b1': _L0_gnn_in['b1'], 'L0_gnn_W2': _L0_gnn_in['W2'], 'L0_gnn_a_src2': _L0_gnn_in['a_src2'], 'L0_gnn_a_dst2': _L0_gnn_in['a_dst2'], 'L0_gnn_b2': _L0_gnn_in['b2'], 'L0_gnn_W_out': _L0_gnn_in['W_out'], 'L0_gnn_b_out': _L0_gnn_in['b_out']}

def reference(x, src, dst, edge_weight1, L0_gnn_W_ah, L0_gnn_b_ah, L0_gnn_W0, L0_gnn_a_src0, L0_gnn_a_dst0, L0_gnn_b0, L0_gnn_W1, L0_gnn_a_src1, L0_gnn_a_dst1, L0_gnn_b1, L0_gnn_W2, L0_gnn_a_src2, L0_gnn_a_dst2, L0_gnn_b2, L0_gnn_W_out, L0_gnn_b_out):
    import jax
    import jax.numpy as jnp

    def _L0_gnn_ref(x, edge_index, batch, edge_attr, W_ah, b_ah, W0, a_src0, a_dst0, b0, W1, a_src1, a_dst1, b1, W2, a_src2, a_dst2, b2, W_out, b_out):
        import jax, jax.numpy as jnp
        import numpy as np
        N, E, D, H, C = (1250, 12500, 768, 4, 192)
        NEG_SLOPE = 0.2

        def gat_conv(x, src, dst, W, a_src, a_dst, b):
            h = (x @ W).reshape(N, H, C)
            as_n = (h * a_src).sum(-1)
            ad_n = (h * a_dst).sum(-1)
            e = jax.nn.leaky_relu(as_n[src] + ad_n[dst], NEG_SLOPE)
            m = jax.ops.segment_max(e, dst, num_segments=N)
            p = jnp.exp(e - m[dst])
            s = jax.ops.segment_sum(p, dst, num_segments=N)
            alpha = p / (s[dst] + 1e-16)
            out = jax.ops.segment_sum(alpha[:, :, None] * h[src], dst, num_segments=N)
            return out.reshape(N, H * C) + b
        loops = jnp.arange(N, dtype=edge_index.dtype)
        src = jnp.concatenate([edge_index[0], loops])
        dst = jnp.concatenate([edge_index[1], loops])
        x1 = jax.nn.relu(x @ W_ah + b_ah)
        xs = [jax.nn.relu(gat_conv(x1, src, dst, W, a_s, a_d, b)) for W, a_s, a_d, b in ((W0, a_src0, a_dst0, b0), (W1, a_src1, a_dst1, b1), (W2, a_src2, a_dst2, b2))]
        node_emb = jnp.concatenate(xs, axis=1)
        return jax.nn.relu(node_emb @ W_out + b_out)
    edge_index = jnp.stack([src, dst])
    batch0 = jnp.zeros((1250,), jnp.int32)
    x = _layernorm(x + _L0_gnn_ref(x, edge_index, batch0, edge_weight1, L0_gnn_W_ah, L0_gnn_b_ah, L0_gnn_W0, L0_gnn_a_src0, L0_gnn_a_dst0, L0_gnn_b0, L0_gnn_W1, L0_gnn_a_src1, L0_gnn_a_dst1, L0_gnn_b1, L0_gnn_W2, L0_gnn_a_src2, L0_gnn_a_dst2, L0_gnn_b2, L0_gnn_W_out, L0_gnn_b_out), axis=-1)
    return x

_drawn_inputs = setup_inputs


def setup_inputs(seed=0):
    import zlib

    import numpy as np

    out = dict(_drawn_inputs(seed))
    spreads = {'L0_gnn_b_ah': (0.0, 0.668),
     'L0_gnn_b0': (0.0, 0.32),
     'L0_gnn_b1': (0.0, 0.341),
     'L0_gnn_b2': (0.0, 0.33),
     'L0_gnn_b_out': (0.0, 0.1)}
    factors = {'L0_gnn_W_ah': 3.906,
     'L0_gnn_a_src0': 8.0,
     'L0_gnn_a_dst0': 29.366,
     'L0_gnn_a_src1': 8.0,
     'L0_gnn_a_dst1': 29.267,
     'L0_gnn_a_src2': 8.0,
     'L0_gnn_a_dst2': 34.837}
    for name, (base, spread) in spreads.items():
        noise = np.random.default_rng([zlib.crc32(name.encode()), seed]).standard_normal(out[name].shape)
        drawn = base * np.exp(spread * noise) if base else spread * noise
        out[name] = jnp.asarray(drawn.astype(out[name].dtype))
    for name, factor in factors.items():
        out[name] = (out[name] * factor).astype(out[name].dtype)
    return out
```

```python
from contextlib import ExitStack

import concourse.bass as bass
from concourse import mybir

N, D = 1250, 768
LAYERS, HEADS = 3, 4
C = D // HEADS
EDGES = 41250
SLOPE = 0.2
EPS = 1e-05

PT = 125
NT = N // PT
KP = 128
KT = D // KP
LH = LAYERS * HEADS
CK = 3
CHUNKS = EDGES // (PT * CK)
AHEAD = CHUNKS
BANK = 512
COLS = [(c, min(BANK, N - c)) for c in range(0, N, BANK)]
GROUPS = [(g, min(4, NT - g)) for g in range(0, NT, 4)]
HALF = D // 2
HW = C + 1
PAIRS = LH // 2
PK = 2 * C // KP
OK = LAYERS * KT
PSLOTS = 4
XSLOTS = 2
NOBODY = -3.0e38
HUGE = 1.0e30


def gnn_program(nc, x, src, dst, W_ah, b_ah, W_all, a_all, b_all, W_out, b_out, out):
    f32, f16, bf16, i32 = mybir.dt.float32, mybir.dt.float16, mybir.dt.bfloat16, mybir.dt.int32
    ALU, ACT, AX = mybir.AluOpType, mybir.ActivationFunctionType, mybir.AxisListType
    ds = bass.ds

    h_dram = nc.dram_tensor("h_dram", (LH, N, C), f32).ap()
    as_dram = nc.dram_tensor("as_dram", (LH, N), f32).ap()
    u_dram = nc.dram_tensor("u_dram", (2 * LH, N), f32).ap()
    xs_dram = nc.dram_tensor("xs_dram", (NT, KP, OK, PT), f32).ap()

    with ExitStack() as ctx:
        def sb(name, shape, dt=f32):
            return ctx.enter_context(nc.sbuf_tensor(name, shape, dt))

        def sem(name):
            return ctx.enter_context(nc.semaphore(name))

        R_CNT = sb("R_CNT", [128, NT * N])
        R_CNTT = sb("R_CNTT", [128, NT * N])
        R_X1 = sb("R_X1", [128, 7600])
        R_W = sb("R_W", [128, OK * D])
        R_SMALL = sb("R_SMALL", [128, 3884])

        def view(region, start, rows, shape, dt=f32):
            size = 1
            for s in shape:
                size *= s
            words = size * (2 if dt in (f16, bf16) else 4) // 4
            v = region[0:rows, start:start + words]
            if dt != f32:
                v = v.bitcast(dt)
            names = "abcd"[:len(shape)]
            if len(shape) > 1:
                v = v.rearrange(f"p ({' '.join(names)}) -> p {' '.join(names)}",
                                **dict(zip(names[1:], shape[1:])))
            return v, start + words

        cnt, _ = view(R_CNT, 0, PT, (NT, N))
        cntT, _ = view(R_CNTT, 0, PT, (NT, N))
        e_int, o = view(R_X1, 0, CHUNKS, (2, CK, PT), i32)
        e_f, o = view(R_X1, o, CHUNKS, (2, CK, PT))
        edgeT, o = view(R_X1, o, PT, (2, CK, CHUNKS))
        span, o = view(R_X1, o, CHUNKS, (2,))
        reach, o = view(R_X1, o, CHUNKS, (4, NT))
        blkpos, o = view(R_X1, o, CHUNKS, (2, NT))
        chunkno, o = view(R_X1, o, CHUNKS, (2,))
        x1T, _ = view(R_X1, 0, KP, (KT, N))
        xin, _ = view(R_CNTT, 0, PT, (NT, D))
        Wv, o = view(R_CNTT, 0, KP, (KT, D))
        Wa, o = view(R_CNTT, o, KP, (KT, D))
        aB, _ = view(R_CNTT, o, KP, (D,))
        W_ah_sb, o = view(R_W, 0, KP, (KT, D))
        xT, _ = view(R_W, o, KP, (KT, N))
        W_sb, _ = view(R_W, 0, KP, (LAYERS, KT, D))
        Wo_sb, _ = view(R_W, 0, KP, (OK, D))
        src1h, o = view(R_SMALL, 0, PT, (CK, N), f16)
        dst1h, o = view(R_SMALL, o, PT, (CK, 128), f16)
        diag, o = view(R_SMALL, o, PT, (2 * N - PT + 1,), f16)
        nodes, _ = view(R_SMALL, o, PT, (N,), f16)
        asB, o = view(R_SMALL, 0, PT, (2, N))
        masked, _ = view(R_SMALL, o, PT, (2, N), bf16)
        z, _ = view(R_SMALL, 2 * N, PT, (2, NT, LH))
        uB, o = view(R_CNT, 0, PT, (2, 2, N))
        expo, o = view(R_CNT, o, PT, (XSLOTS, N))
        prob, _ = view(R_CNT, o, PT, (PSLOTS, N))
        hB, _ = view(R_SMALL, 0, PT, (2, NT, HW))
        att, o = view(R_X1, 0, PT, (NT, 2 * C))
        xsT, _ = view(R_X1, o, KP, (PK, N))
        xsn, o = view(R_CNT, 0, KP, (3, OK, PT))
        boB, o = view(R_CNT, o, PT, (D,))
        xres, o = view(R_CNTT, 0, PT, (NT, D))
        yt, o = view(R_CNTT, o, PT, (2, D))
        yo, _ = view(R_CNTT, o, PT, (2, D))

        h_out = sb("h_out", [PT, 2, D])
        ident = sb("ident", [128, 128])
        ident16 = diag[:, N - PT:N]
        zero16 = diag[:, 0:PT]
        before = sb("before", [NT, NT])
        V = sb("V", [KP, KT, 2 * LH])
        asad = sb("asad", [PT, NT, 2 * LH])
        s08 = sb("s08", [PT, NT, LH])
        s02 = sb("s02", [PT, NT, LH])
        amax = sb("amax", [PT, NT, LH])
        u = sb("u", [PT, NT, 2 * LH])
        asT = h_out[0:LH].rearrange("p a f -> p (a f)")[:, 0:N]
        b_ah_sb = sb("b_ah_sb", [KP, KT])
        b_all_sb = sb("b_all_sb", [KP, OK])
        b_pair = sb("b_pair", [KP, PK])
        rsum = sb("rsum", [PT, 2, NT])
        rinv = sb("rinv", [PT, 2, NT])
        ab = sb("ab", [NT, 3])
        table = sb("table", [1, 3, NT], i32)
        stats = sb("stats", [PT, 2, 6])
        mv = sb("mv", [PT, 2, 2])
        rstd = sb("rstd", [PT, 2, 2])
        epsc = sb("epsc", [PT, 1])
        uT, _ = view(R_SMALL, 0, 2 * LH, (N,))

        ps = ctx.enter_context(nc.psum_tensor("ps", [128, 8 * BANK], f32))
        bank = lambda b: ps[:, b * BANK:(b + 1) * BANK]

        names = """edges_in x_in wah_in small_in consts_made edges_f edgesT_ps edgesT_sb reach_sb reachT_ps
            ab_sb rows_ps table_sb xT_ps xT_sb onehot_ready onehot_free acc_ready acc_free
            wv_in wa_made wv_free v_made x1_ps x1_sb asad_ps asad_sb asT_ps asT_sb as_stored
            cntT_ps cntT_sb masked_done max_made mask_ready scores_ready b_pair_sb uT_ps uT_sb u_stored
            w_in h_ps h_sb x_ready exp_done p_ready p_used hB_free
            rsum_sb rinv_sb out_evac attT_ps attT_sb xs_stored xs_free u_used wo_in
            res_in y_ps y_sum stat_done std_done yo_ready chain pchain amax_done h_all""".split()
        S = {n: sem(n) for n in names}
        asB_in = [sem("asB_in0"), sem("asB_in1")]
        h_stored = [sem("h_stored0"), sem("h_stored1")]
        uB_in = [sem("uB_in0"), sem("uB_in1")]
        hB_in = [sem("hB_in0"), sem("hB_in1")]
        xsn_in = [sem(f"xsn_in{i}") for i in range(3)]
        out_stored = [sem("out_stored0"), sem("out_stored1")]

        block = ctx.enter_context(nc.Block())

        @block.sync
        def _(sp):
            sp.dma_start(e_int[:, 0], dst.rearrange("(c k e) -> c k e", k=CK, e=PT)).then_inc(S["edges_in"], 16)
            sp.dma_start(e_int[:, 1], src.rearrange("(c k e) -> c k e", k=CK, e=PT)).then_inc(S["edges_in"], 16)
            sp.dma_start(xin, x.rearrange("(t p) f -> p t f", p=PT)).then_inc(S["x_in"], 16)
            sp.dma_start(W_ah_sb, W_ah.rearrange("(k p) f -> p k f", p=KP)).then_inc(S["wah_in"], 16)
            sp.dma_start(b_ah_sb[:], b_ah).then_inc(S["small_in"], 16)
            sp.dma_start(b_all_sb[:], b_all).then_inc(S["small_in"], 16)

            sp.wait_ge(S["xT_ps"], KT * len(GROUPS))
            for l in range(LAYERS):
                if l > 0:
                    sp.wait_ge(S["wv_free"], 2 * l)
                sp.dma_start(Wv, W_all[l].rearrange("(k p) f -> p k f", p=KP)).then_inc(S["wv_in"], 16)
                for which in range(2):
                    if l > 0 or which > 0:
                        sp.wait_ge(S["wa_made"], 2 * l + which)
                    sp.dma_start(aB, a_all[l, which:which + 1].broadcast_to((KP, D))).then_inc(S["wv_in"], 16)

            sp.wait_ge(S["x1_ps"], KT)
            for l in range(LAYERS):
                sp.dma_start(W_sb[:, l], W_all[l].rearrange("(k p) f -> p k f", p=KP)).then_inc(S["w_in"], 16)

            sp.wait_ge(S["asT_sb"], len(GROUPS))
            sp.dma_start(as_dram, asT[:]).then_inc(S["as_stored"], 16)
            sp.wait_ge(S["as_stored"], 16)
            sp.wait_ge(S["acc_ready"], NT)
            for hh in range(LH):
                if hh >= 2:
                    sp.wait_ge(S["max_made"], NT * (hh - 1))
                sp.dma_start(asB[:, hh % 2], as_dram[hh:hh + 1].broadcast_to((PT, N))).then_inc(asB_in[hh % 2], 16)

            sp.wait_ge(S["uT_sb"], len(GROUPS))
            sp.dma_start(u_dram, uT).then_inc(S["u_stored"], 16)
            sp.wait_ge(S["u_stored"], 16)
            sp.wait_ge(S["h_all"], 1)
            uu = u_dram.rearrange("(w h) n -> h w n", w=2)
            with sp.Fori(0, PAIRS) as p:
                for q in range(2):
                    sp.wait_ge(S["u_used"], 2 * p + q + 1)
                    sp.dma_start(uB[:, q], uu[ds(2 * p + q, 1)].broadcast_to((PT, 2, N))).then_inc(uB_in[q], 16)
                    sp.wait_ge(S["hB_free"], 2 * p + q + 1)
                    sp.dma_start(hB[:, q, :, 0:C],
                                 h_dram[ds(2 * p + q, 1)].rearrange("o (t n) c -> n (o t) c", n=PT)
                                 ).then_inc(hB_in[q], 16)

            sp.wait_ge(S["xs_stored"], 16 * PK * PAIRS)
            sp.wait_ge(S["p_used"], PSLOTS + NT * LH)
            def store(t):
                sp.wait_ge(S["yo_ready"], t + 1)
                sp.dma_start(out[t * PT:(t + 1) * PT], yo[:, t % 2]).then_inc(out_stored[t % 2], 16)

            for t in range(NT):
                if t >= 3:
                    sp.wait_ge(S["y_ps"], t - 2)
                sp.dma_start(xsn[:, t % 3], xs_dram[t]).then_inc(xsn_in[t % 3], 16)
                if t == 0:
                    sp.dma_start(xres, x.rearrange("(t p) f -> p t f", p=PT)).then_inc(S["res_in"], 16)
                    sp.dma_start(boB, b_out.broadcast_to((PT, D))).then_inc(S["res_in"], 16)
                if t >= 3:
                    store(t - 3)
            for t in range(NT - 3, NT):
                store(t)
            sp.wait_ge(out_stored[0], 16 * (NT // 2))
            sp.wait_ge(out_stored[1], 16 * (NT // 2))

        @block.gpsimd
        def _(pool):
            n = [0]

            def link(ins):
                n[0] += 1
                ins.then_inc(S["pchain"], 1)
                pool.wait_ge(S["pchain"], n[0])

            link(nc.gpsimd.memset(ident[:], 0.0))
            link(nc.gpsimd.affine_select(out=ident[:], in_=ident[:], compare_op=ALU.not_equal, fill=1.0,
                                         base=0, pattern=[[-1, 128]], channel_multiplier=1))
            link(nc.gpsimd.memset(before[:], 1.0))
            link(nc.gpsimd.affine_select(out=before[:], in_=before[:], compare_op=ALU.is_gt, fill=0.0,
                                         base=0, pattern=[[1, NT]], channel_multiplier=-1))
            link(nc.gpsimd.memset(diag, 0.0))
            link(nc.gpsimd.tensor_copy(ident16, ident[0:PT, 0:PT]))
            link(nc.gpsimd.iota(nodes, pattern=[[1, N]], base=0, channel_multiplier=0,
                                allow_small_or_imprecise_dtypes=True))
            link(nc.gpsimd.iota(blkpos[:, 0], pattern=[[PT, NT]], base=0, channel_multiplier=0,
                                allow_small_or_imprecise_dtypes=True))
            link(nc.gpsimd.iota(blkpos[:, 1], pattern=[[PT, NT]], base=PT - 1, channel_multiplier=0,
                                allow_small_or_imprecise_dtypes=True))
            link(nc.gpsimd.iota(chunkno[:, 0:1], pattern=[[0, 1]], base=CHUNKS, channel_multiplier=-1,
                                allow_small_or_imprecise_dtypes=True))
            nc.gpsimd.iota(chunkno[:, 1:2], pattern=[[0, 1]], base=1, channel_multiplier=1,
                           allow_small_or_imprecise_dtypes=True).then_inc(S["consts_made"], 1)

            for l in range(LAYERS):
                for which in range(2):
                    pool.wait_ge(S["wv_in"], 16 * (3 * l + 2 + which))
                    if l + which > 0:
                        pool.wait_ge(S["v_made"], 2 * l + which)
                    last = nc.gpsimd.tensor_tensor(Wa, Wv, aB.rearrange("p (o f) -> p o f", o=1).broadcast_to((KP, KT, D)),
                                                   ALU.mult)
                    last.then_inc(S["wa_made"], 1)
                    pool.wait_ge(S["wa_made"], 2 * l + which + 1)
                    if which == 1:
                        pool.sem_inc(S["wv_free"], 2)
                    prod = Wa.rearrange("p k (h c) -> p (k h) c", c=C)
                    w = C
                    while w % 2 == 0:
                        w //= 2
                        link(nc.gpsimd.tensor_tensor(prod[:, :, 0:w], prod[:, :, 0:w], prod[:, :, w:2 * w], ALU.add))
                    link(nc.gpsimd.tensor_tensor(prod[:, :, 0:1], prod[:, :, 0:1], prod[:, :, 1:2], ALU.add))
                    o = which * LH + l * HEADS
                    nc.gpsimd.tensor_tensor(V[:, :, o:o + HEADS], Wa.rearrange("p k (h c) -> p k h c", c=C)[:, :, :, 0],
                                            Wa.rearrange("p k (h c) -> p k h c", c=C)[:, :, :, 2],
                                            ALU.add).then_inc(S["v_made"], 1)

            pool.wait_ge(S["u_stored"], 16)
            nc.gpsimd.memset(hB[:, :, :, C:HW], 1.0).then_inc(S["hB_free"], 2)
            pool.wait_ge(S["h_ps"], LAYERS * NT)
            pool.dma_start(Wo_sb, W_out.rearrange("(k p) f -> p k f", p=KP)).then_inc(S["wo_in"], 16)

            pool.sem_inc(S["xs_free"], 1)
            with pool.Fori(0, PAIRS) as p:
                pool.wait_ge(S["attT_sb"], 9 * p + 10)
                for k in range(PK):
                    pool.dma_start(xs_dram.rearrange("t p k n -> p k t n")[:, ds(PK * p + k, 1)],
                                   xsT[:, k].rearrange("p (o t n) -> p o t n", o=1, n=PT)).then_inc(S["xs_stored"], 16)
                pool.wait_ge(S["xs_stored"], 16 * PK * (p + 1))
                pool.sem_inc(S["xs_free"], 1)

        @block.scalar
        def _(act):
            i = 0
            for k in range(KT):
                for g, w in GROUPS:
                    act.wait_ge(S["xT_ps"], i + 1)
                    nc.scalar.copy(xT[:, k, g * PT:(g + w) * PT], bank(4 + i % 4)[:, 0:w * PT]).then_inc(S["xT_sb"], 1)
                    i += 1
            with act.Fori(0, NT // 2) as b2:
                for half in range(2):
                    act.wait_ge(S["acc_ready"], 2 * b2 + half + 1)
                    nc.scalar.copy(cnt[:, ds(2 * b2 + half, 1)],
                                   ps[0:PT, half * 3 * BANK:half * 3 * BANK + N].rearrange("p (o n) -> p o n", o=1)
                                   ).then_inc(S["acc_free"], 1)
            act.wait_ge(S["small_in"], 32)
            for m in range(KT):
                act.wait_ge(S["x1_ps"], m + 1)
                o = (m % 2) * 3 * BANK
                nc.scalar.activation(x1T[:, m], ps[:, o:o + N], ACT.Relu, bias=b_ah_sb[:, m:m + 1]).then_inc(S["x1_sb"], 1)
            for i, (g, w) in enumerate(GROUPS):
                act.wait_ge(S["asT_ps"], i + 1)
                nc.scalar.copy(asT[:, g * PT:(g + w) * PT], bank(i)[0:LH, 0:w * PT]).then_inc(S["asT_sb"], 1)
            act.wait_ge(S["v_made"], 2 * LAYERS)
            i = 0
            for j in range(NT):
                for g, w in GROUPS:
                    act.wait_ge(S["cntT_ps"], i + 1)
                    nc.scalar.copy(cntT[:, j, g * PT:(g + w) * PT], bank(i % 4)[0:PT, 0:w * PT]).then_inc(S["cntT_sb"], 1)
                    i += 1
            act.wait_ge(S["as_stored"], 16)
            act.sem_inc(h_stored[0], 16)
            act.sem_inc(h_stored[1], 16)
            with act.Fori(0, LAYERS) as l:
                for t in range(NT):
                    act.wait_ge(S["h_ps"], NT * l + t + 1)
                    act.wait_ge(h_stored[t % 2], 16 * (NT // 2 * l + t // 2 + 1))
                    nc.scalar.copy(h_out[:, t % 2].rearrange("p (c f) -> p c f", c=2),
                                   ps[0:PT, (t % 2) * 2 * BANK:(t % 2 + 1) * 2 * BANK]
                                   .rearrange("p (c f) -> p c f", c=2)[:, :, 0:HALF]).then_inc(S["h_sb"], 1)
                    act.wait_ge(S["h_sb"], NT * l + t + 3)
                    act.dma_start(h_dram.rearrange("(l h) n c -> n l h c", l=LAYERS)[t * PT:(t + 1) * PT, ds(l, 1)],
                                  h_out[:, t % 2].rearrange("p (o h c) -> p o h c", o=1, h=HEADS)
                                  ).then_inc(h_stored[t % 2], 16)
            act.wait_ge(h_stored[0], 16 * (LAYERS * NT // 2 + 1))
            act.wait_ge(h_stored[1], 16 * (LAYERS * NT // 2 + 1))
            act.sem_inc(S["h_all"], 1)
            act.wait_ge(S["amax_done"], 1)
            for i, (g, w) in enumerate(GROUPS):
                act.wait_ge(S["uT_ps"], i + 1)
                nc.scalar.copy(uT[:, g * PT:(g + w) * PT], bank(5 + i)[0:2 * LH, 0:w * PT]).then_inc(S["uT_sb"], 1)

            def exp_tile(p, r):
                n = 2 * NT * p + r
                act.wait_ge(S["x_ready"], n + 1)
                act.wait_ge(S["p_used"], n + 1)
                act.wait_ge(S["scores_ready"], 1)
                nc.scalar.activation(prob[:, r % PSLOTS], expo[:, r % XSLOTS], ACT.Exp,
                                     bias=s02[:, r % NT, ds(2 * p + r // NT, 1)]).then_inc(S["exp_done"], 1)

            def pair(p, last):
                for r in range(2 * NT):
                    if r >= 2:
                        exp_tile(p, r)
                    if r % NT == NT - 1:
                        q = r // NT
                        if q == 0 or not last:
                            nxt = (p, r + 1) if q == 0 else (p + 1, 0)
                            if q == 1:
                                exp_tile(nxt[0], 0)
                                exp_tile(nxt[0], 1)
                        act.wait_ge(S["rinv_sb"], 2 * p + q + 1)
                        if q == 0:
                            act.wait_ge(S["attT_ps"], 9 * p + 1)
                        for t in range(NT):
                            o = (t // 2) * BANK + (t % 2) * 256
                            nc.scalar.activation(att[:, t, q * C:(q + 1) * C], ps[0:PT, o:o + C], ACT.Copy,
                                                 scale=rinv[:, q, t:t + 1]).then_inc(S["out_evac"], 1)
                nc.scalar.copy(b_pair[:], b_all_sb[:, ds(PK * p, PK)]).then_inc(S["b_pair_sb"], 1)
                act.wait_ge(S["b_pair_sb"], p + 1)
                act.wait_ge(S["xs_free"], p + 1)
                i = 0
                for k in range(PK):
                    for g, w in GROUPS:
                        act.wait_ge(S["attT_ps"], 9 * p + i + 2)
                        nc.scalar.activation(xsT[:, k, g * PT:(g + w) * PT], bank(5 + i % 3)[:, 0:w * PT], ACT.Relu,
                                             bias=b_pair[:, k:k + 1]).then_inc(S["attT_sb"], 1)
                        i += 1

            act.sem_inc(S["exp_done"], XSLOTS)
            act.sem_inc(S["out_evac"], NT)
            act.sem_inc(S["attT_sb"], 1)
            exp_tile(0, 0)
            exp_tile(0, 1)
            with act.Fori(0, PAIRS - 1) as p:
                pair(p, False)
            pair(PAIRS - 1, True)

            for t in range(NT):
                act.wait_ge(S["stat_done"], t + 1)
                nc.scalar.activation(rstd[:, t % 2, 0:1], mv[:, t % 2, 1:2], ACT.Sqrt, bias=epsc[:, 0:1]).then_inc(S["std_done"], 1)

        @block.vector
        def _(dve):
            n = [0]

            def link(ins):
                n[0] += 1
                ins.then_inc(S["chain"], 1)
                dve.wait_ge(S["chain"], n[0])

            nc.vector.memset(epsc[:], EPS)
            dve.wait_ge(S["edges_in"], 32)
            link(nc.vector.tensor_copy(e_f[:, 0], e_int[:, 0]))
            nc.vector.tensor_copy(e_f[:, 1], e_int[:, 1]).then_inc(S["edges_f"], 1)
            link(nc.vector.tensor_reduce(span[:, 0:1], e_f[:, 0], axis=AX.XY, op=ALU.min))
            link(nc.vector.tensor_reduce(span[:, 1:2], e_f[:, 0], axis=AX.XY, op=ALU.max))
            dve.wait_ge(S["consts_made"], 1)
            link(nc.vector.tensor_scalar(reach[:, 0], blkpos[:, 1], span[:, 0:1], None, ALU.is_ge))
            link(nc.vector.tensor_scalar(reach[:, 1], blkpos[:, 0], span[:, 1:2], None, ALU.is_le))
            link(nc.vector.tensor_tensor(reach[:, 0], reach[:, 0], reach[:, 1], ALU.mult))
            link(nc.vector.tensor_scalar(reach[:, 2], reach[:, 0], chunkno[:, 0:1], None, ALU.mult))
            nc.vector.tensor_scalar(reach[:, 3], reach[:, 0], chunkno[:, 1:2], None, ALU.mult).then_inc(S["reach_sb"], 1)
            for which in range(2):
                dve.wait_ge(S["edgesT_ps"], which + 1)
                nc.vector.tensor_copy(edgeT[:, which], bank(which)[0:PT, 0:CK * CHUNKS]
                                      .rearrange("p (k c) -> p k c", k=CK)).then_inc(S["edgesT_sb"], 1)
            dve.wait_ge(S["reachT_ps"], 1)
            link(nc.vector.tensor_reduce(ab[:, 0:2], bank(2)[0:NT, 0:256].rearrange("p (w c) -> p w c", w=2)[:, :, 0:CHUNKS],
                                         axis=AX.X, op=ALU.max))
            link(nc.vector.tensor_scalar(ab[:, 0:1], ab[:, 0:1], 1.0, None, ALU.max))
            link(nc.vector.tensor_scalar(ab[:, 2:3], ab[:, 0:1], -1.0, CHUNKS + 1.0, ALU.mult, ALU.add))
            link(nc.vector.tensor_tensor(ab[:, 1:2], ab[:, 1:2], ab[:, 2:3], ALU.max))
            link(nc.vector.tensor_tensor(ab[:, 2:3], ab[:, 0:1], ab[:, 1:2], ALU.add))
            nc.vector.tensor_scalar(ab[:, 2:3], ab[:, 2:3], -float(CHUNKS), None, ALU.add).then_inc(S["ab_sb"], 1)
            dve.wait_ge(S["rows_ps"], 1)
            nc.vector.tensor_scalar(table[0:1, 0], bank(3)[0:1, 0:NT], -1.0, float(CHUNKS), ALU.mult, ALU.add)
            link(nc.vector.tensor_copy(table[0:1, 1:3], bank(3)[0:1, NT:3 * NT].rearrange("p (a b) -> p a b", a=2)))
            dve.sem_inc(S["table_sb"], 1)

            dve.sem_inc(S["onehot_ready"], CK * AHEAD)
            with dve.Fori(0, NT) as b:
                first = dve.value_load(table[0:1, 0, ds(b, 1)], min_val=0, max_val=CHUNKS - 1)
                end = dve.value_load(table[0:1, 1, ds(b, 1)], min_val=1, max_val=CHUNKS)
                ahead = dve.value_load(table[0:1, 2, ds(b, 1)], min_val=0, max_val=AHEAD + CHUNKS * NT)
                with dve.Fori(first, end) as c:
                    g = ahead + c
                    for k in range(CK):
                        dve.wait_ge(S["onehot_free"], CK * g + k + 1)
                        nc.vector.tensor_scalar(dst1h[:, k, 0:PT], nodes[:, ds(b * PT, PT)],
                                                edgeT[:, 0, k, ds(c, 1)], None, ALU.is_equal)
                        nc.vector.tensor_scalar(src1h[:, k], nodes, edgeT[:, 1, k, ds(c, 1)], None,
                                                ALU.is_equal).then_inc(S["onehot_ready"], 1)

            dve.wait_ge(S["asad_ps"], 1)
            link(nc.vector.tensor_copy(asad[:], bank(7)[0:PT, 0:NT * 2 * LH].rearrange("p (t h) -> p t h", t=NT)))
            dve.sem_inc(S["asad_sb"], 1)
            nc.vector.tensor_scalar(s08[:], asad[:, :, 0:LH], 1.0 - SLOPE, None, ALU.mult)
            link(nc.vector.tensor_scalar(s02[:], asad[:, :, 0:LH], SLOPE, None, ALU.mult))
            dve.sem_inc(S["scores_ready"], 1)
            dve.wait_ge(S["cntT_ps"], NT * len(GROUPS))
            for b in range(NT):
                nc.vector.tensor_scalar(cnt[:, b], cnt[:, b], 0.0, NOBODY, ALU.is_equal, ALU.mult
                                        ).then_inc(S["mask_ready"], 1)
            dve.wait_ge(S["mask_ready"], NT)
            for hh in range(LH):
                dve.wait_ge(asB_in[hh % 2], 16 * (hh // 2 + 1))
                for b in range(NT):
                    i = NT * hh + b
                    if i >= 2:
                        dve.wait_ge(S["max_made"], i - 1)
                    nc.vector.tensor_tensor_reduce(out=masked[:, i % 2], in0=cnt[:, b], in1=asB[:, hh % 2], scale=1.0,
                                                   scalar=NOBODY, op0=ALU.add, op1=ALU.max,
                                                   accum_out=amax[:, b, hh:hh + 1]).then_inc(S["max_made"], 1)
            dve.wait_ge(S["max_made"], LH * NT)
            ad = asad[:, :, LH:2 * LH]
            link(nc.vector.tensor_tensor(z[:, 0], amax[:], ad, ALU.add))
            link(nc.vector.tensor_scalar(z[:, 1], z[:, 0], SLOPE, None, ALU.mult))
            link(nc.vector.tensor_tensor(z[:, 0], z[:, 0], z[:, 1], ALU.max))
            link(nc.vector.tensor_scalar(z[:, 1], ad, SLOPE, None, ALU.mult))
            link(nc.vector.tensor_tensor(u[:, :, 0:LH], ad, z[:, 0], ALU.subtract))
            link(nc.vector.tensor_tensor(u[:, :, LH:2 * LH], z[:, 1], z[:, 0], ALU.subtract))
            dve.sem_inc(S["amax_done"], 1)
            dve.sem_inc(S["u_used"], 2)

            def exponent_tile(p, r):
                n = 2 * NT * p + r
                q = r // NT
                if r % NT == 0:
                    dve.wait_ge(uB_in[q], 16 * p + 16)
                dve.wait_ge(S["exp_done"], n + 1)
                nc.vector.scalar_tensor_tensor(out=expo[:, r % XSLOTS], in0=uB[:, q, 0],
                                               scalar=s08[:, r % NT, ds(2 * p + q, 1)], in1=uB[:, q, 1],
                                               op0=ALU.add, op1=ALU.max).then_inc(S["x_ready"], 1)
                if r % NT == NT - 1:
                    dve.wait_ge(S["x_ready"], n + 1)
                    dve.sem_inc(S["u_used"], 1)

            def pair(p, last):
                for r in range(2 * NT):
                    n = 2 * NT * p + r
                    if r + XSLOTS < 2 * NT:
                        exponent_tile(p, r + XSLOTS)
                    elif not last:
                        exponent_tile(p + 1, r + XSLOTS - 2 * NT)
                    dve.wait_ge(S["exp_done"], n + XSLOTS + 1)
                    nc.vector.scalar_tensor_tensor(out=prob[:, r % PSLOTS], in0=prob[:, r % PSLOTS], scalar=HUGE,
                                                   in1=cntT[:, r % NT], op0=ALU.min, op1=ALU.mult
                                                   ).then_inc(S["p_ready"], 1)
                    if r % NT == NT - 1:
                        q = r // NT
                        dve.wait_ge(S["p_used"], n + PSLOTS + 1)
                        dve.wait_ge(S["out_evac"], NT * (2 * p + q + 1))
                        nc.vector.tensor_scalar(rsum[:, q], ps[0:PT, 0:NT * 256].rearrange("p (t w) -> p t w", w=256)[:, :, C],
                                                1e-16, None, ALU.add).then_inc(S["rsum_sb"], 1)
                        dve.wait_ge(S["rsum_sb"], 2 * p + q + 1)
                        nc.vector.reciprocal(rinv[:, q], rsum[:, q]).then_inc(S["rinv_sb"], 1)

            exponent_tile(0, 0)
            exponent_tile(0, 1)
            with dve.Fori(0, PAIRS - 1) as p:
                pair(p, False)
            pair(PAIRS - 1, True)

            dve.wait_ge(S["res_in"], 32)
            for t in range(NT):
                i = t % 2
                dve.wait_ge(S["y_ps"], t + 1)
                y_ps = ps[0:PT, i * 2 * BANK:(i + 1) * 2 * BANK].rearrange("p (c f) -> p c f", c=2)[:, :, 0:HALF]
                ins = nc.vector.tensor_tensor(yt[:, i].rearrange("p (c f) -> p c f", c=2), y_ps,
                                              boB.rearrange("p (c f) -> p c f", c=2), ALU.add)
                ins.then_inc(S["y_sum"], 1)
                dve.wait_ge(S["y_sum"], t + 1)
                link(nc.vector.scalar_tensor_tensor(out=yt[:, i], in0=yt[:, i], scalar=0.0, in1=xres[:, t],
                                                    op0=ALU.max, op1=ALU.add))
                for c in range(2):
                    ins = nc.vector.bn_stats(stats[:, c], yt[:, i, c * HALF:(c + 1) * HALF])
                link(ins)
                nc.vector.bn_aggr(mv[:, i], stats[:].rearrange("p c s -> p (c s)")).then_inc(S["stat_done"], 1)
                dve.wait_ge(S["std_done"], t + 1)
                link(nc.vector.reciprocal(rstd[:, i, 1:2], rstd[:, i, 0:1]))
                if t >= 2:
                    dve.wait_ge(out_stored[i], 16 * (t // 2))
                nc.vector.tensor_scalar(yo[:, i], yt[:, i], mv[:, i, 0:1], rstd[:, i, 1:2], ALU.subtract,
                                        ALU.mult).then_inc(S["yo_ready"], 1)

        @block.tensor
        def _(pe):
            mm = nc.tensor.matmul
            pe.wait_ge(S["consts_made"], 1)
            pe.wait_ge(S["edges_f"], 1)
            for which in range(2):
                for k in range(CK):
                    ins = nc.tensor.transpose(bank(which)[0:PT, k * CHUNKS:(k + 1) * CHUNKS], e_f[:, which, k],
                                              ident[0:CHUNKS, 0:CHUNKS])
                ins.then_inc(S["edgesT_ps"], 1)
            pe.wait_ge(S["reach_sb"], 1)
            for w in range(2):
                ins = nc.tensor.transpose(bank(2)[0:NT, w * 128:w * 128 + CHUNKS], reach[:, 2 + w],
                                          ident[0:CHUNKS, 0:CHUNKS])
            ins.then_inc(S["reachT_ps"], 1)
            pe.wait_ge(S["x_in"], 16)
            i = 0
            for k in range(KT):
                for g, w in GROUPS:
                    if i >= 4:
                        pe.wait_ge(S["xT_sb"], i - 3)
                    for t in range(w):
                        ins = nc.tensor.transpose(bank(4 + i % 4)[:, t * PT:(t + 1) * PT],
                                                  xin[:, g + t, k * KP:(k + 1) * KP], ident[0:PT, 0:PT])
                    ins.then_inc(S["xT_ps"], 1)
                    i += 1
            pe.wait_ge(S["ab_sb"], 1)
            mm(bank(3)[0:1, 0:NT], ab[:, 0:1], ident[0:NT, 0:NT], start=True, stop=True)
            mm(bank(3)[0:1, NT:2 * NT], ab[:, 1:2], ident[0:NT, 0:NT], start=True, stop=True)
            mm(bank(3)[0:1, 2 * NT:3 * NT], ab[:, 2:3], before[:], start=True, stop=False)
            mm(bank(3)[0:1, 2 * NT:3 * NT], ab[:, 0:1], ident[0:NT, 0:NT], start=False, stop=True).then_inc(S["rows_ps"], 1)
            pe.wait_ge(S["table_sb"], 1)
            pe.wait_ge(S["edgesT_sb"], 2)
            pe.wait_ge(S["xT_sb"], KT * len(GROUPS))

            pe.sem_inc(S["onehot_free"], CK * AHEAD + CK)
            pe.sem_inc(S["acc_free"], 2)
            with pe.Fori(0, NT // 2) as b2:
                for half in range(2):
                    b = 2 * b2 + half
                    acc = ps[0:PT, half * 3 * BANK:half * 3 * BANK + N]
                    first = pe.value_load(table[0:1, 0, ds(b, 1)], min_val=0, max_val=CHUNKS - 1)
                    end = pe.value_load(table[0:1, 1, ds(b, 1)], min_val=1, max_val=CHUNKS)
                    ahead = pe.value_load(table[0:1, 2, ds(b, 1)], min_val=0, max_val=AHEAD + CHUNKS * NT)
                    pe.wait_ge(S["acc_free"], b + 1)
                    for o, w in COLS:
                        mm(acc[:, o:o + w], ident16, diag[:, ds((N - PT) - b * PT + o, w)], start=True, stop=False,
                           skip_group_check=True)
                    with pe.Fori(first, end) as c:
                        g = ahead + c
                        for k in range(CK):
                            pe.wait_ge(S["onehot_ready"], CK * g + k + 1)
                            for o, w in COLS:
                                ins = mm(acc[:, o:o + w], dst1h[:, k, 0:PT], src1h[:, k, o:o + w], start=False,
                                         stop=False, skip_group_check=True)
                            ins.then_inc(S["onehot_free"], 1)
                    for o, w in COLS:
                        ins = mm(acc[:, o:o + 2], zero16, diag[:, 0:2], start=False, stop=True,
                                 skip_group_check=True)
                    ins.then_inc(S["acc_ready"], 1)

            pe.wait_ge(S["wah_in"], 16)
            pe.wait_ge(S["acc_free"], 2 + NT)
            for m in range(KT):
                if m >= 2:
                    pe.wait_ge(S["x1_sb"], m - 1)
                for k in range(KT):
                    for o, w in COLS:
                        oo = (m % 2) * 3 * BANK + o
                        ins = mm(ps[:, oo:oo + w], W_ah_sb[:, k, m * KP:(m + 1) * KP], xT[:, k, o:o + w],
                                 start=(k == 0), stop=(k == KT - 1))
                ins.then_inc(S["x1_ps"], 1)
            pe.wait_ge(S["x1_sb"], KT)
            pe.wait_ge(S["v_made"], 2 * LAYERS)
            for t in range(NT):
                for k in range(KT):
                    ins = mm(bank(7)[0:PT, t * 2 * LH:(t + 1) * 2 * LH], x1T[:, k, t * PT:(t + 1) * PT], V[:, k],
                             start=(k == 0), stop=(k == KT - 1))
            ins.then_inc(S["asad_ps"], 1)
            pe.wait_ge(S["asad_sb"], 1)
            for i, (g, w) in enumerate(GROUPS):
                for t in range(w):
                    ins = nc.tensor.transpose(bank(i)[0:LH, t * PT:(t + 1) * PT], asad[:, g + t, 0:LH], ident[0:PT, 0:PT])
                ins.then_inc(S["asT_ps"], 1)
            pe.wait_ge(S["asT_sb"], len(GROUPS))
            i = 0
            for j in range(NT):
                for g, w in GROUPS:
                    if i >= 4:
                        pe.wait_ge(S["cntT_sb"], i - 3)
                    for t in range(w):
                        ins = nc.tensor.transpose(bank(i % 4)[0:PT, t * PT:(t + 1) * PT],
                                                  cnt[:, g + t, j * PT:(j + 1) * PT], ident[0:PT, 0:PT])
                    ins.then_inc(S["cntT_ps"], 1)
                    i += 1
            pe.wait_ge(S["cntT_sb"], NT * len(GROUPS))
            pe.wait_ge(S["w_in"], 16 * LAYERS)
            pe.sem_inc(S["h_sb"], 2)
            with pe.Fori(0, LAYERS) as l:
                for t in range(NT):
                    pe.wait_ge(S["h_sb"], NT * l + t + 1)
                    for k in range(KT):
                        for c in range(2):
                            o = (t % 2 * 2 + c) * BANK
                            ins = mm(ps[0:PT, o:o + HALF].rearrange("p (o f) -> p o f", o=1), x1T[:, k, t * PT:(t + 1) * PT],
                                     W_sb[:, ds(l, 1), k, c * HALF:(c + 1) * HALF],
                                     start=(k == 0), stop=(k == KT - 1))
                    ins.then_inc(S["h_ps"], 1)
            pe.wait_ge(S["amax_done"], 1)
            for i, (g, w) in enumerate(GROUPS):
                for t in range(w):
                    ins = nc.tensor.transpose(bank(5 + i)[0:2 * LH, t * PT:(t + 1) * PT], u[:, g + t], ident[0:PT, 0:PT])
                ins.then_inc(S["uT_ps"], 1)

            pe.wait_ge(S["uT_sb"], len(GROUPS))
            pe.wait_ge(S["h_sb"], 2 + LAYERS * NT)
            pe.sem_inc(S["p_used"], PSLOTS)
            pe.sem_inc(S["attT_ps"], 1)
            with pe.Fori(0, PAIRS) as p:
                for q in range(2):
                    pe.wait_ge(hB_in[q], 16 * p + 16)
                    for j in range(NT):
                        r = q * NT + j
                        pe.wait_ge(S["p_ready"], 2 * NT * p + r + 1)
                        for t in range(NT):
                            if j == 0 and t % 2 == 0:
                                pe.wait_ge(S["out_evac"], NT * (2 * p + q) + t + 2)
                            o = t * 256
                            ins = mm(ps[0:PT, o:o + HW], prob[:, r % PSLOTS, t * PT:(t + 1) * PT], hB[:, q, j],
                                     start=(j == 0 and t % 2 == 0), stop=(j == NT - 1), skip_group_check=True)
                        ins.then_inc(S["p_used"], 1)
                    pe.wait_ge(S["p_used"], 2 * NT * p + q * NT + NT + PSLOTS)
                    pe.sem_inc(S["hB_free"], 1)
                pe.wait_ge(S["out_evac"], NT * (2 * p + 2) + NT)
                i = 0
                for k in range(PK):
                    for g, w in GROUPS:
                        pe.wait_ge(S["attT_sb"], 9 * p + 1 + max(i - 2, 0))
                        for t in range(w):
                            ins = nc.tensor.transpose(bank(5 + i % 3)[:, t * PT:(t + 1) * PT],
                                                      att[:, g + t, k * KP:(k + 1) * KP], ident[0:PT, 0:PT])
                        ins.then_inc(S["attT_ps"], 1)
                        i += 1

            pe.wait_ge(S["wo_in"], 16)
            for t in range(NT):
                pe.wait_ge(xsn_in[t % 3], 16 * (t // 3 + 1))
                if t >= 2:
                    pe.wait_ge(S["y_sum"], t - 1)
                for k in range(OK):
                    for c in range(2):
                        o = (t % 2 * 2 + c) * BANK
                        ins = mm(ps[0:PT, o:o + HALF], xsn[:, t % 3, k], Wo_sb[:, k, c * HALF:(c + 1) * HALF],
                                 start=(k == 0), stop=(k == OK - 1))
                ins.then_inc(S["y_ps"], 1)


_OUT = (N, D)


def kernel(**inputs):
    import numpy as np
    import concourse.bacc as bacc
    from concourse.bass_utils import run_bass_kernel_spmd

    i = {k: np.asarray(v) for k, v in inputs.items()}
    p = "L0_gnn_"
    arrays = {
        "x": i["x"], "src": i["src"], "dst": i["dst"],
        "W_ah": i[p + "W_ah"],
        "b_ah": i[p + "b_ah"].reshape(KT, KP).T,
        "W_all": np.stack([i[f"{p}W{l}"] for l in range(LAYERS)]),
        "a_all": np.stack([np.stack([i[f"{p}a_src{l}"].reshape(D), i[f"{p}a_dst{l}"].reshape(D)])
                           for l in range(LAYERS)]),
        "b_all": np.stack([i[f"{p}b{l}"] for l in range(LAYERS)]).reshape(OK, KP).T,
        "W_out": i[p + "W_out"],
        "b_out": i[p + "b_out"].reshape(1, D),
    }
    arrays = {f"in_{k}": np.ascontiguousarray(v) for k, v in arrays.items()}
    nc = bacc.Bacc("TRN2", target_bir_lowering=False, num_devices=1)
    args = [nc.dram_tensor(k, v.shape, mybir.dt.from_np(v.dtype), kind="ExternalInput").ap()
            for k, v in arrays.items()]
    args.append(nc.dram_tensor("out_0", _OUT, mybir.dt.float32, kind="ExternalOutput").ap())
    gnn_program(nc, *args)
    r = run_bass_kernel_spmd(nc, [arrays], core_ids=[0])
    return r.results[0]["out_0"]
```

```python
from contextlib import ExitStack

import concourse.bass as bass
from concourse import mybir

N, D = 1250, 768
LAYERS, HEADS = 3, 4
C = D // HEADS
EDGES = 41250
SLOPE = 0.2
EPS = 1e-05

PT = 125
NT = N // PT
KP = 128
KT = D // KP
LH = LAYERS * HEADS
CK = 3
CHUNKS = EDGES // (PT * CK)
DSLOTS = 4
SPARE = 8
AHEAD = CHUNKS + SPARE
BANK = 512
COLS = [(c, min(BANK, N - c)) for c in range(0, N, BANK)]
GROUPS = [(g, min(4, NT - g)) for g in range(0, NT, 4)]
HALF = D // 2
HW = C + 1
PAIRS = LH // 2
FEAT = 6
EARLY = 2
U_AT = 5
PK = 2 * C // KP
OK = LAYERS * KT
PSLOTS = 4
XSLOTS = 2
VSLOTS = 5
NOBODY = -3.0e38
HUGE = 1.0e30


def gnn_program(nc, x, src, dst, W_ah, b_ah, W_all, a_all, b_all, W_out, b_out, out):
    f32, f16, bf16, i32 = mybir.dt.float32, mybir.dt.float16, mybir.dt.bfloat16, mybir.dt.int32
    ALU, ACT, AX = mybir.AluOpType, mybir.ActivationFunctionType, mybir.AxisListType
    ds = bass.ds

    h_dram = nc.dram_tensor("h_dram", (LH, N, C), f32).ap()
    as_dram = nc.dram_tensor("as_dram", (LH, N), f32).ap()
    u_dram = nc.dram_tensor("u_dram", (2 * LH, N), f32).ap()
    xs_dram = nc.dram_tensor("xs_dram", (NT, KP, OK, PT), f32).ap()

    with ExitStack() as ctx:
        def sb(name, shape, dt=f32):
            return ctx.enter_context(nc.sbuf_tensor(name, shape, dt))

        def sem(name):
            return ctx.enter_context(nc.semaphore(name))

        R_CNT = sb("R_CNT", [128, NT * N])
        R_CNTT = sb("R_CNTT", [128, NT * N])
        R_X1 = sb("R_X1", [128, 7600])
        R_W = sb("R_W", [128, OK * D])
        R_SMALL = sb("R_SMALL", [128, 4072])

        def view(region, start, rows, shape, dt=f32):
            size = 1
            for s in shape:
                size *= s
            words = size * (2 if dt in (f16, bf16) else 4) // 4
            v = region[0:rows, start:start + words]
            if dt != f32:
                v = v.bitcast(dt)
            names = "abcd"[:len(shape)]
            if len(shape) > 1:
                v = v.rearrange(f"p ({' '.join(names)}) -> p {' '.join(names)}",
                                **dict(zip(names[1:], shape[1:])))
            return v, start + words

        cnt, _ = view(R_CNT, 0, PT, (NT, N))
        cntT, _ = view(R_CNTT, 0, PT, (NT, N))
        e_int, o = view(R_X1, 0, CHUNKS, (2, CK, PT), i32)
        e_f, o = view(R_X1, o, CHUNKS, (2, CK, PT))
        edgeT, o = view(R_X1, o, PT, (2, CK, CHUNKS + 2))
        span, o = view(R_X1, o, CHUNKS, (2,))
        reach, o = view(R_X1, o, CHUNKS, (4, NT))
        blkpos, o = view(R_X1, o, CHUNKS, (2, NT))
        chunkno, o_dist = view(R_X1, o, CHUNKS, (2,))
        x1T, _ = view(R_X1, 0, KP, (KT, N))
        xin, _ = view(R_CNTT, 0, PT, (NT, D))
        Wv, o = view(R_SMALL, 0, KP, (VSLOTS, D))
        Wa, _ = view(R_SMALL, o, KP, (2, C), bf16)
        W_ah_sb, o = view(R_W, 0, KP, (KT, D))
        xT, _ = view(R_W, o, KP, (KT, N))
        W_sb, _ = view(R_W, 0, KP, (LAYERS, KT, D))
        Wo_sb, _ = view(R_W, 0, KP, (OK, D))
        src1h, o = view(R_SMALL, 0, PT, (CK, N), f16)
        dst1h, o = view(R_SMALL, o, PT, (2, CK, 128), f16)
        diag, o = view(R_SMALL, o, PT, (2 * N - PT + 1,), f16)
        nodes, _ = view(R_SMALL, o, PT, (N,), f16)
        dist, _ = view(R_X1, o_dist, PT, (DSLOTS, CK, PT))
        asB, o = view(R_SMALL, 0, PT, (2, N))
        masked, _ = view(R_SMALL, o, PT, (2, N), bf16)
        z, _ = view(R_SMALL, 2 * N, PT, (2, NT, LH))
        uB, o = view(R_CNT, 0, PT, (2, 2, N))
        expo, o = view(R_CNT, o, PT, (XSLOTS, N))
        prob, _ = view(R_CNT, o, PT, (PSLOTS, N))
        hB, _ = view(R_SMALL, 0, PT, (2, NT, HW))
        att, o = view(R_X1, 0, PT, (NT, 2 * C))
        xsT, _ = view(R_X1, o, KP, (PK, N))
        xsn = [view(R_CNT, 2 * N * i, KP, (OK, PT))[0] for i in range(3)]
        xres, o = view(R_CNTT, 0, PT, (NT, D))
        yt, o = view(R_CNTT, o, PT, (2, D))
        yo, o = view(R_CNTT, o, PT, (2, D))
        boB, _ = view(R_CNTT, o, PT, (D,))

        h_outs = sb("h_out", [128, 2, D])
        h_out = h_outs[0:PT]
        aB = h_outs
        ident = sb("ident", [128, 128])
        ident16 = diag[:, N - PT:N]
        zero16 = diag[:, 0:PT]
        before = sb("before", [NT, NT])
        u_place = sb("u_place", [128, NT * 2 * LH])
        u = u_place[0:PT].rearrange("p (t h) -> p t h", t=NT)
        V = u_place[:, 0:KT * 2 * LH].rearrange("p (k h) -> p k h", k=KT)
        asad = sb("asad", [PT, NT, 2 * LH])
        s08 = sb("s08", [PT, NT, LH])
        s02 = sb("s02", [PT, NT, LH])
        amax = sb("amax", [PT, NT, LH])
        asadT = h_outs[0:2 * LH].rearrange("p a f -> p (a f)")[:, 0:N]
        b_ah_sb = sb("b_ah_sb", [KP, KT])
        b_all_sb = sb("b_all_sb", [KP, OK])
        b_pair = sb("b_pair", [KP, PK])
        rsum = sb("rsum", [PT, 2, NT])
        rinv = sb("rinv", [PT, 2, NT])
        ab = sb("ab", [NT, 3])
        table = sb("table", [1, 3, NT], i32)
        stats = sb("stats", [PT, 2, 6])
        mv = sb("mv", [PT, 2, 2])
        rstd = sb("rstd", [PT, 2, 2])
        epsc = sb("epsc", [PT, 1])
        uT, _ = view(R_SMALL, 0, 2 * LH, (N,))

        ps = ctx.enter_context(nc.psum_tensor("ps", [128, 8 * BANK], f32))
        bank = lambda b: ps[:, b * BANK:(b + 1) * BANK]

        names = """edges_in x_in wah_in small_in consts_made edges_f edgesT_ps edgesT_sb reach_sb reachT_ps
            ab_sb rows_ps table_sb xT_ps xT_even xT_odd dst_ready dist_done onehot_ready onehot_free acc_ready acc_free
            v_made x1_ps x1_sb asad_ps asadT_ps asadT_sb as_stored
            cntT_ps cntT_sb masked_done max_made mask_ready scores_ready b_pair_sb uT_ps uT_sb u_stored
            w_in h_ps h_sb x_ready exp_done p_ready p_used hB_ones
            rsum_sb rinv_sb out_evac attT_ps attT_sb xs_stored xs_free u_used wo_in
            res_in y_ps y_sum stat_done std_done yo_ready chain pchain amax_done""".split()
        S = {n: sem(n) for n in names}
        asB_in = [sem("asB_in0"), sem("asB_in1")]
        h_stored = [sem("h_stored0"), sem("h_stored1")]
        uB_in = [sem("uB_in0"), sem("uB_in1")]
        hB_in = [sem("hB_in0"), sem("hB_in1")]
        xsn_early = [sem(f"xsn_early{i}") for i in range(3)]
        xsn_late = [sem(f"xsn_late{i}") for i in range(3)]
        a_in = [sem(f"a_in{l}") for l in range(LAYERS)]
        wv_in = [sem(f"wv_in{i}") for i in range(VSLOTS)]
        out_stored = [sem("out_stored0"), sem("out_stored1")]

        block = ctx.enter_context(nc.Block())

        @block.sync
        def _(sp):
            sp.dma_start(e_int[:, 0], dst.rearrange("(c k e) -> c k e", k=CK, e=PT)).then_inc(S["edges_in"], 16)
            sp.dma_start(e_int[:, 1], src.rearrange("(c k e) -> c k e", k=CK, e=PT)).then_inc(S["edges_in"], 16)
            sp.dma_start(xin, x.rearrange("(t p) f -> p t f", p=PT)).then_inc(S["x_in"], 16)
            sp.dma_start(W_ah_sb, W_ah.rearrange("(k p) f -> p k f", p=KP)).then_inc(S["wah_in"], 16)
            sp.dma_start(b_ah_sb[:], b_ah).then_inc(S["small_in"], 16)
            sp.dma_start(b_all_sb[:], b_all).then_inc(S["small_in"], 16)

            sp.wait_ge(S["acc_ready"], NT)
            for l in range(LAYERS):
                if l > 0:
                    sp.wait_ge(S["v_made"], 2 * HEADS * KT * l)
                sp.dma_start(aB[:].rearrange("p w f -> p (w f)"),
                             a_all[l:l + 1].rearrange("l w f -> l (w f)").broadcast_to((KP, 2 * D))).then_inc(a_in[l], 16)
                for k in range(KT):
                    i = KT * l + k
                    if i >= VSLOTS:
                        sp.wait_ge(S["v_made"], 2 * HEADS * (i - VSLOTS + 1))
                    sp.dma_start(Wv[:, i % VSLOTS], W_all[l, k * KP:(k + 1) * KP]).then_inc(wv_in[i % VSLOTS], 16)

            sp.wait_ge(S["x1_ps"], KT)
            for l in range(LAYERS):
                sp.dma_start(W_sb[:, l], W_all[l].rearrange("(k p) f -> p k f", p=KP)).then_inc(S["w_in"], 16)
                if l == 0:
                    sp.wait_ge(S["asadT_sb"], 1)
                    sp.dma_start(as_dram, asadT[0:LH]).then_inc(S["as_stored"], 16)
                    sp.wait_ge(S["as_stored"], 16)
                    for hh in range(2):
                        sp.dma_start(asB[:, hh], as_dram[hh:hh + 1].broadcast_to((PT, N))).then_inc(asB_in[hh], 16)
                if l + 1 < LAYERS:
                    sp.wait_ge(S["w_in"], 16 * (l + 1))

            for hh in range(2, LH):
                sp.wait_ge(S["max_made"], NT * (hh - 1))
                sp.dma_start(asB[:, hh % 2], as_dram[hh:hh + 1].broadcast_to((PT, N))).then_inc(asB_in[hh % 2], 16)

            sp.wait_ge(S["uT_sb"], len(GROUPS))
            sp.dma_start(u_dram, uT).then_inc(S["u_stored"], 16)
            sp.wait_ge(S["u_stored"], 16)
            uu = u_dram.rearrange("(w h) n -> h w n", w=2)

            def load_u(p, q):
                sp.dma_start(uB[:, q], uu[ds(2 * p + q, 1)].broadcast_to((PT, 2, N))).then_inc(uB_in[q], 16)

            def load_h(p, q):
                sp.dma_start(hB[:, q, :, 0:C], h_dram[ds(2 * p + q, 1)].rearrange("o (t n) c -> n (o t) c", n=PT)
                             ).then_inc(hB_in[q], 16)

            for q in range(2):
                load_u(0, q)
            sp.wait_ge(h_stored[0], 16 * (NT // 2 + 1))
            sp.wait_ge(h_stored[1], 16 * (NT // 2 + 1))
            sp.wait_ge(S["hB_ones"], 1)
            for q in range(2):
                load_h(0, q)
            sp.wait_ge(h_stored[0], 16 * (LAYERS * NT // 2 + 1))
            sp.wait_ge(h_stored[1], 16 * (LAYERS * NT // 2 + 1))
            with sp.Fori(1, PAIRS) as p:
                for q in range(2):
                    sp.wait_ge(S["u_used"], 2 * p + q - 1)
                    load_u(p, q)
                    sp.wait_ge(S["p_used"], PSLOTS + NT * (2 * p + q - 1))
                    load_h(p, q)

            early = OK - PK
            sp.wait_ge(S["xs_stored"], 16 * PK * (PAIRS - 1))

            def load_early(t):
                sp.dma_start(xsn[t % 3][:, 0:early], xs_dram[t, :, 0:early]).then_inc(xsn_early[t % 3], 16)

            def load_late(t):
                sp.dma_start(xsn[t % 3][:, early:OK], xs_dram[t, :, early:OK]).then_inc(xsn_late[t % 3], 16)

            def store(t):
                sp.wait_ge(S["yo_ready"], t + 1)
                sp.dma_start(out[t * PT:(t + 1) * PT], yo[:, t % 2]).then_inc(out_stored[t % 2], 16)

            sp.wait_ge(S["u_used"], LH - 1)
            load_early(0)
            sp.wait_ge(S["u_used"], LH)
            load_early(1)
            sp.wait_ge(S["exp_done"], XSLOTS + LH * NT)
            load_early(2)
            sp.wait_ge(S["p_used"], PSLOTS + LH * NT)
            sp.dma_start(xres, x.rearrange("(t p) f -> p t f", p=PT)).then_inc(S["res_in"], 16)
            sp.dma_start(boB, b_out.broadcast_to((PT, D))).then_inc(S["res_in"], 16)
            sp.wait_ge(S["xs_stored"], 16 * PK * PAIRS)
            for t in range(3):
                load_late(t)
            for t in range(NT):
                if t >= 3:
                    sp.wait_ge(S["y_ps"], t - 2)
                    load_early(t)
                    load_late(t)
                    store(t - 3)
            for t in range(NT - 3, NT):
                store(t)
            sp.wait_ge(out_stored[0], 16 * (NT // 2))
            sp.wait_ge(out_stored[1], 16 * (NT // 2))

        @block.gpsimd
        def _(pool):
            n = [0]

            def link(ins):
                n[0] += 1
                ins.then_inc(S["pchain"], 1)
                pool.wait_ge(S["pchain"], n[0])

            link(nc.gpsimd.memset(ident[:], 0.0))
            link(nc.gpsimd.affine_select(out=ident[:], in_=ident[:], compare_op=ALU.not_equal, fill=1.0,
                                         base=0, pattern=[[-1, 128]], channel_multiplier=1))
            link(nc.gpsimd.memset(before[:], 1.0))
            link(nc.gpsimd.affine_select(out=before[:], in_=before[:], compare_op=ALU.is_gt, fill=0.0,
                                         base=0, pattern=[[1, NT]], channel_multiplier=-1))
            link(nc.gpsimd.memset(diag, 0.0))
            link(nc.gpsimd.tensor_copy(ident16, ident[0:PT, 0:PT]))
            link(nc.gpsimd.iota(nodes, pattern=[[1, N]], base=0, channel_multiplier=0,
                                allow_small_or_imprecise_dtypes=True))
            link(nc.gpsimd.iota(blkpos[:, 0], pattern=[[PT, NT]], base=0, channel_multiplier=0,
                                allow_small_or_imprecise_dtypes=True))
            link(nc.gpsimd.iota(blkpos[:, 1], pattern=[[PT, NT]], base=PT - 1, channel_multiplier=0,
                                allow_small_or_imprecise_dtypes=True))
            link(nc.gpsimd.iota(chunkno[:, 0:1], pattern=[[0, 1]], base=CHUNKS, channel_multiplier=-1,
                                allow_small_or_imprecise_dtypes=True))
            nc.gpsimd.iota(chunkno[:, 1:2], pattern=[[0, 1]], base=1, channel_multiplier=1,
                           allow_small_or_imprecise_dtypes=True).then_inc(S["consts_made"], 1)

            pool.wait_ge(S["u_stored"], 16)
            nc.gpsimd.memset(hB[:, :, :, C:HW], 1.0).then_inc(S["hB_ones"], 1)
            pool.wait_ge(S["p_used"], PSLOTS + NT)
            pool.dma_start(Wo_sb, W_out.rearrange("(k p) f -> p k f", p=KP)).then_inc(S["wo_in"], 16)

            pool.sem_inc(S["xs_free"], 1)
            with pool.Fori(0, PAIRS) as p:
                for k in range(PK):
                    pool.wait_ge(S["attT_sb"], 9 * p + 3 * k + 4)
                    pool.dma_start(xs_dram.rearrange("t p k n -> p k t n")[:, ds(PK * p + k, 1)],
                                   xsT[:, k].rearrange("p (o t n) -> p o t n", o=1, n=PT)).then_inc(S["xs_stored"], 16)
                pool.wait_ge(S["xs_stored"], 16 * PK * (p + 1))
                pool.sem_inc(S["xs_free"], 1)

        @block.scalar
        def _(act):
            act.wait_ge(S["table_sb"], 1)
            act.wait_ge(S["edgesT_sb"], 2)
            act.sem_inc(S["dst_ready"], AHEAD + DSLOTS)

            def distances(b, c, g):
                act.wait_ge(S["dst_ready"], g + 1)
                act.wait_ge(S["edgesT_sb"], 2)
                for k in range(CK):
                    nc.scalar.activation(dist[:, ds(g % DSLOTS, 1), k], nodes[:, ds(b * PT, PT)].rearrange("p (o n) -> p o n", o=1),
                                         ACT.Abs, bias=edgeT[:, 0, k, ds(c, 1)], scale=-1.0).then_inc(S["dist_done"], 1)

            def dst_onehots(b):
                first = act.value_load(table[0:1, 0, ds(b, 1)], min_val=0, max_val=CHUNKS - 1)
                end = act.value_load(table[0:1, 1, ds(b, 1)], min_val=1, max_val=CHUNKS)
                ahead = act.value_load(table[0:1, 2, ds(b, 1)], min_val=SPARE, max_val=AHEAD + CHUNKS * NT)
                act.wait_ge(S["dist_done"], CK * (ahead + first + b))
                distances(b, first, ahead + first)
                with act.Fori(first, end) as c:
                    g = ahead + c
                    distances(b, c + 1, g + 1)
                    act.wait_ge(S["dist_done"], CK * (g + b) + CK)
                    act.wait_ge(S["onehot_free"], CK * g)
                    act.wait_ge(S["edgesT_sb"], 2)
                    nc.scalar.activation(dst1h[:, ds(g % 2, 1), :, 0:PT].rearrange("p o k n -> p (o k) n"),
                                         dist[:, ds(g % DSLOTS, 1)].rearrange("p o k n -> p (o k) n"),
                                         ACT.Relu, bias=1.0, scale=-1.0).then_inc(S["dst_ready"], 1)

            def counts_out(b2, half):
                act.wait_ge(S["acc_ready"], 2 * b2 + half + 1)
                nc.scalar.copy(cnt[:, ds(2 * b2 + half, 1)],
                               ps[0:PT, half * 3 * BANK:half * 3 * BANK + N].rearrange("p (o n) -> p o n", o=1)
                               ).then_inc(S["acc_free"], 1)

            act.sem_inc(S["dist_done"], CK * AHEAD)
            dst_onehots(0)
            with act.Fori(0, NT // 2 - 1) as b2:
                for half in range(2):
                    dst_onehots(2 * b2 + half + 1)
                    counts_out(b2, half)
            dst_onehots(NT - 1)
            for half in range(2):
                counts_out(NT // 2 - 1, half)
            for i in range(0, KT * len(GROUPS), 2):
                k, (g, w) = i // len(GROUPS), GROUPS[i % len(GROUPS)]
                act.wait_ge(S["xT_ps"], i + 1)
                nc.scalar.copy(xT[:, k, g * PT:(g + w) * PT], bank(4 + i % 4)[:, 0:w * PT]).then_inc(S["xT_even"], 1)
            act.wait_ge(S["small_in"], 32)
            for step in range(KT * KT):
                if step < NT * len(GROUPS):
                    j, (g, w) = step // len(GROUPS), GROUPS[step % len(GROUPS)]
                    act.wait_ge(S["cntT_ps"], step + 1)
                    nc.scalar.copy(cntT[:, j, g * PT:(g + w) * PT], bank(6 + step % 2)[0:PT, 0:w * PT]
                                   ).then_inc(S["cntT_sb"], 1)
                if step % KT == KT - 1:
                    m = step // KT
                    act.wait_ge(S["x1_ps"], m + 1)
                    o = (m % 2) * 3 * BANK
                    nc.scalar.activation(x1T[:, m], ps[:, o:o + N], ACT.Relu, bias=b_ah_sb[:, m:m + 1]
                                         ).then_inc(S["x1_sb"], 1)
            act.wait_ge(S["v_made"], 2 * HEADS * KT * LAYERS)
            act.wait_ge(S["asadT_ps"], 1)
            nc.scalar.copy(asadT, ps[0:2 * LH, 0:N]).then_inc(S["asadT_sb"], 1)
            act.wait_ge(S["as_stored"], 16)
            act.wait_ge(S["asad_ps"], 1)
            act.sem_inc(h_stored[0], 16)
            act.sem_inc(h_stored[1], 16)

            def h_tile(l, t):
                act.wait_ge(S["h_ps"], NT * l + t + 1)
                act.wait_ge(h_stored[t % 2], 16 * (NT // 2 * l + t // 2 + 1))
                nc.scalar.copy(h_out[:, t % 2].rearrange("p (c f) -> p c f", c=2),
                               ps[0:PT, (t % 2) * 2 * BANK:(t % 2 + 1) * 2 * BANK]
                               .rearrange("p (c f) -> p c f", c=2)[:, :, 0:HALF]).then_inc(S["h_sb"], 1)
                act.wait_ge(S["h_sb"], NT * l + t + 3)
                act.dma_start(h_dram.rearrange("(l h) n c -> n l h c", l=LAYERS)[t * PT:(t + 1) * PT, ds(l, 1)],
                              h_out[:, t % 2].rearrange("p (o h c) -> p o h c", o=1, h=HEADS)
                              ).then_inc(h_stored[t % 2], 16)

            with act.Fori(0, LAYERS - 1) as l:
                for t in range(NT):
                    h_tile(l, t)
            for t in range(NT):
                h_tile(LAYERS - 1, t)
                if t == U_AT:
                    for i, (g, w) in enumerate(GROUPS):
                        act.wait_ge(S["uT_ps"], i + 1)
                        nc.scalar.copy(uT[:, g * PT:(g + w) * PT], bank(5 + i)[0:2 * LH, 0:w * PT]
                                       ).then_inc(S["uT_sb"], 1)

            def exp_tile(p, r):
                p, r = p + r // (2 * NT), r % (2 * NT)
                n = 2 * NT * p + r
                act.wait_ge(S["x_ready"], n + 1)
                act.wait_ge(S["p_used"], n + 1)
                act.wait_ge(S["scores_ready"], 1)
                nc.scalar.activation(prob[:, r % PSLOTS], expo[:, r % XSLOTS], ACT.Exp,
                                     bias=s02[:, r % NT, ds(2 * p + r // NT, 1)]).then_inc(S["exp_done"], 1)

            def head_out(p, q):
                act.wait_ge(S["rinv_sb"], 2 * p + q + 1)
                if q == 0:
                    act.wait_ge(S["attT_ps"], 9 * p + 1)
                for t in range(NT):
                    o = (t // 2) * BANK + (t % 2) * 256
                    nc.scalar.activation(att[:, t, q * C:(q + 1) * C], ps[0:PT, o:o + C], ACT.Copy,
                                         scale=rinv[:, q, t:t + 1]).then_inc(S["out_evac"], 1)

            def features(p, k):
                if k == 0:
                    act.wait_ge(S["xs_free"], p + 1)
                    nc.scalar.copy(b_pair[:], b_all_sb[:, ds(PK * p, PK)]).then_inc(S["b_pair_sb"], 1)
                    act.wait_ge(S["b_pair_sb"], p + 1)
                for i, (g, w) in enumerate(GROUPS):
                    act.wait_ge(S["attT_ps"], 9 * p + 3 * k + i + 2)
                    nc.scalar.activation(xsT[:, k, g * PT:(g + w) * PT], bank(5 + i)[:, 0:w * PT], ACT.Relu,
                                         bias=b_pair[:, k:k + 1]).then_inc(S["attT_sb"], 1)

            def pair(p, last):
                for r in range(NT, 2 * NT if last else 3 * NT):
                    exp_tile(p, r)
                    if r == NT + EARLY:
                        head_out(p, 0)
                    if r == 2 * NT + EARLY:
                        head_out(p, 1)
                    if not last and r >= 3 * NT - PK:
                        features(p, r - (3 * NT - PK))
                if last:
                    head_out(p, 1)
                    for k in range(PK):
                        features(p, k)

            act.sem_inc(S["exp_done"], XSLOTS)
            act.sem_inc(S["out_evac"], NT)
            act.sem_inc(S["attT_sb"], 1)
            for r in range(NT):
                exp_tile(0, r)
            with act.Fori(0, PAIRS - 1) as p:
                pair(p, False)
            pair(PAIRS - 1, True)

            for t in range(NT):
                act.wait_ge(S["stat_done"], t + 1)
                nc.scalar.activation(rstd[:, t % 2, 0:1], mv[:, t % 2, 1:2], ACT.Sqrt, bias=epsc[:, 0:1]).then_inc(S["std_done"], 1)

        @block.vector
        def _(dve):
            n = [0]

            def link(ins):
                n[0] += 1
                ins.then_inc(S["chain"], 1)
                dve.wait_ge(S["chain"], n[0])

            nc.vector.memset(epsc[:], EPS)
            dve.wait_ge(S["edges_in"], 32)
            link(nc.vector.tensor_copy(e_f[:, 0], e_int[:, 0]))
            nc.vector.tensor_copy(e_f[:, 1], e_int[:, 1]).then_inc(S["edges_f"], 1)
            link(nc.vector.tensor_reduce(span[:, 0:1], e_f[:, 0], axis=AX.XY, op=ALU.min))
            link(nc.vector.tensor_reduce(span[:, 1:2], e_f[:, 0], axis=AX.XY, op=ALU.max))
            dve.wait_ge(S["consts_made"], 1)
            link(nc.vector.tensor_scalar(reach[:, 0], blkpos[:, 1], span[:, 0:1], None, ALU.is_ge))
            link(nc.vector.tensor_scalar(reach[:, 1], blkpos[:, 0], span[:, 1:2], None, ALU.is_le))
            link(nc.vector.tensor_tensor(reach[:, 0], reach[:, 0], reach[:, 1], ALU.mult))
            link(nc.vector.tensor_scalar(reach[:, 2], reach[:, 0], chunkno[:, 0:1], None, ALU.mult))
            nc.vector.tensor_scalar(reach[:, 3], reach[:, 0], chunkno[:, 1:2], None, ALU.mult).then_inc(S["reach_sb"], 1)
            nc.vector.memset(edgeT[:, 0, :, CHUNKS:CHUNKS + 2], -1.0)
            for which in range(2):
                dve.wait_ge(S["edgesT_ps"], which + 1)
                nc.vector.tensor_copy(edgeT[:, which, :, 0:CHUNKS], bank(which)[0:PT, 0:CK * CHUNKS]
                                      .rearrange("p (k c) -> p k c", k=CK)).then_inc(S["edgesT_sb"], 1)
            dve.wait_ge(S["reachT_ps"], 1)
            link(nc.vector.tensor_reduce(ab[:, 0:2], bank(2)[0:NT, 0:256].rearrange("p (w c) -> p w c", w=2)[:, :, 0:CHUNKS],
                                         axis=AX.X, op=ALU.max))
            link(nc.vector.tensor_scalar(ab[:, 0:1], ab[:, 0:1], 1.0, None, ALU.max))
            link(nc.vector.tensor_scalar(ab[:, 2:3], ab[:, 0:1], -1.0, CHUNKS + 1.0, ALU.mult, ALU.add))
            link(nc.vector.tensor_tensor(ab[:, 1:2], ab[:, 1:2], ab[:, 2:3], ALU.max))
            link(nc.vector.tensor_tensor(ab[:, 2:3], ab[:, 0:1], ab[:, 1:2], ALU.add))
            nc.vector.tensor_scalar(ab[:, 2:3], ab[:, 2:3], -float(CHUNKS), None, ALU.add).then_inc(S["ab_sb"], 1)
            dve.wait_ge(S["rows_ps"], 1)
            nc.vector.tensor_scalar(table[0:1, 0], bank(3)[0:1, 0:NT], -1.0, float(CHUNKS), ALU.mult, ALU.add)
            nc.vector.tensor_copy(table[0:1, 1], bank(3)[0:1, NT:2 * NT])
            link(nc.vector.tensor_scalar(table[0:1, 2], bank(3)[0:1, 2 * NT:3 * NT], float(SPARE), None, ALU.add))
            dve.sem_inc(S["table_sb"], 1)

            dve.sem_inc(S["onehot_ready"], CK * AHEAD)
            with dve.Fori(0, NT) as b:
                first = dve.value_load(table[0:1, 0, ds(b, 1)], min_val=0, max_val=CHUNKS - 1)
                end = dve.value_load(table[0:1, 1, ds(b, 1)], min_val=1, max_val=CHUNKS)
                ahead = dve.value_load(table[0:1, 2, ds(b, 1)], min_val=SPARE, max_val=AHEAD + CHUNKS * NT)
                with dve.Fori(first, end) as c:
                    g = ahead + c
                    for k in range(CK):
                        dve.wait_ge(S["onehot_free"], CK * g + k + 1)
                        nc.vector.tensor_scalar(src1h[:, k], nodes, edgeT[:, 1, k, ds(c, 1)], None,
                                                ALU.is_equal).then_inc(S["onehot_ready"], 1)

            for i in range(1, KT * len(GROUPS), 2):
                k, (g, w) = i // len(GROUPS), GROUPS[i % len(GROUPS)]
                dve.wait_ge(S["xT_ps"], i + 1)
                nc.vector.tensor_copy(xT[:, k, g * PT:(g + w) * PT], bank(4 + i % 4)[:, 0:w * PT]).then_inc(S["xT_odd"], 1)
            for l in range(LAYERS):
                dve.wait_ge(a_in[l], 16)
                for k in range(KT):
                    i = KT * l + k
                    dve.wait_ge(wv_in[i % VSLOTS], 16 * (i // VSLOTS + 1))
                    for w in range(2):
                        for h in range(HEADS):
                            m = 2 * HEADS * i + HEADS * w + h
                            col = w * LH + l * HEADS + h
                            if m >= 2:
                                dve.wait_ge(S["v_made"], m - 1)
                            nc.vector.tensor_tensor_reduce(out=Wa[:, m % 2], in0=Wv[:, i % VSLOTS, h * C:(h + 1) * C],
                                                           in1=aB[:, w, h * C:(h + 1) * C], scale=1.0, scalar=0.0,
                                                           op0=ALU.mult, op1=ALU.add, accum_out=V[:, k, col:col + 1]
                                                           ).then_inc(S["v_made"], 1)
            dve.wait_ge(S["cntT_ps"], NT * len(GROUPS))
            for b in range(NT):
                nc.vector.tensor_scalar(cnt[:, b], cnt[:, b], 0.0, NOBODY, ALU.is_equal, ALU.mult
                                        ).then_inc(S["mask_ready"], 1)
            dve.wait_ge(S["asad_ps"], 1)
            link(nc.vector.tensor_copy(asad[:], bank(7)[0:PT, 0:NT * 2 * LH].rearrange("p (t h) -> p t h", t=NT)))
            nc.vector.tensor_scalar(s08[:], asad[:, :, 0:LH], 1.0 - SLOPE, None, ALU.mult)
            link(nc.vector.tensor_scalar(s02[:], asad[:, :, 0:LH], SLOPE, None, ALU.mult))
            dve.sem_inc(S["scores_ready"], 1)
            dve.wait_ge(S["mask_ready"], NT)
            for hh in range(LH):
                dve.wait_ge(asB_in[hh % 2], 16 * (hh // 2 + 1))
                for b in range(NT):
                    i = NT * hh + b
                    if i >= 2:
                        dve.wait_ge(S["max_made"], i - 1)
                    nc.vector.tensor_tensor_reduce(out=masked[:, i % 2], in0=cnt[:, b], in1=asB[:, hh % 2], scale=1.0,
                                                   scalar=NOBODY, op0=ALU.add, op1=ALU.max,
                                                   accum_out=amax[:, b, hh:hh + 1]).then_inc(S["max_made"], 1)
            dve.wait_ge(S["max_made"], LH * NT)
            ad = asad[:, :, LH:2 * LH]
            link(nc.vector.tensor_tensor(z[:, 0], amax[:], ad, ALU.add))
            link(nc.vector.tensor_scalar(z[:, 1], z[:, 0], SLOPE, None, ALU.mult))
            link(nc.vector.tensor_tensor(z[:, 0], z[:, 0], z[:, 1], ALU.max))
            link(nc.vector.tensor_scalar(z[:, 1], ad, SLOPE, None, ALU.mult))
            link(nc.vector.tensor_tensor(u[:, :, 0:LH], ad, z[:, 0], ALU.subtract))
            link(nc.vector.tensor_tensor(u[:, :, LH:2 * LH], z[:, 1], z[:, 0], ALU.subtract))
            dve.sem_inc(S["amax_done"], 1)

            def exponent_tile(p, r):
                p, r = p + r // (2 * NT), r % (2 * NT)
                n = 2 * NT * p + r
                q = r // NT
                if r % NT == 0:
                    dve.wait_ge(uB_in[q], 16 * p + 16)
                dve.wait_ge(S["exp_done"], n + 1)
                nc.vector.scalar_tensor_tensor(out=expo[:, r % XSLOTS], in0=uB[:, q, 0],
                                               scalar=s08[:, r % NT, ds(2 * p + q, 1)], in1=uB[:, q, 1],
                                               op0=ALU.add, op1=ALU.max).then_inc(S["x_ready"], 1)
                if r % NT == NT - 1:
                    dve.wait_ge(S["x_ready"], n + 1)
                    dve.sem_inc(S["u_used"], 1)

            def weight_tile(p, r):
                p, r = p + r // (2 * NT), r % (2 * NT)
                dve.wait_ge(S["exp_done"], 2 * NT * p + r + XSLOTS + 1)
                nc.vector.scalar_tensor_tensor(out=prob[:, r % PSLOTS], in0=prob[:, r % PSLOTS], scalar=HUGE,
                                               in1=cntT[:, r % NT], op0=ALU.min, op1=ALU.mult
                                               ).then_inc(S["p_ready"], 1)

            def invert(p, q):
                dve.wait_ge(S["p_used"], 2 * NT * p + NT * (q + 1) + PSLOTS)
                dve.wait_ge(S["out_evac"], NT * (2 * p + q + 1))
                nc.vector.tensor_scalar(rsum[:, q], ps[0:PT, 0:NT * 256].rearrange("p (t w) -> p t w", w=256)[:, :, C],
                                        1e-16, None, ALU.add).then_inc(S["rsum_sb"], 1)
                dve.wait_ge(S["rsum_sb"], 2 * p + q + 1)
                nc.vector.reciprocal(rinv[:, q], rsum[:, q]).then_inc(S["rinv_sb"], 1)

            def pair(p, last):
                for r in range(EARLY + 1, (2 * NT if last else 2 * NT + EARLY + 1)):
                    if not (last and r + XSLOTS >= 2 * NT):
                        exponent_tile(p, r + XSLOTS)
                    weight_tile(p, r)
                    if r == NT + EARLY:
                        invert(p, 0)
                invert(p, 1)

            for r in range(XSLOTS):
                exponent_tile(0, r)
            for r in range(EARLY + 1):
                exponent_tile(0, r + XSLOTS)
                weight_tile(0, r)
            with dve.Fori(0, PAIRS - 1) as p:
                pair(p, False)
            pair(PAIRS - 1, True)

            dve.wait_ge(S["res_in"], 32)
            for t in range(NT):
                i = t % 2
                dve.wait_ge(S["y_ps"], t + 1)
                y_ps = ps[0:PT, i * 2 * BANK:(i + 1) * 2 * BANK].rearrange("p (c f) -> p c f", c=2)[:, :, 0:HALF]
                ins = nc.vector.tensor_tensor(yt[:, i].rearrange("p (c f) -> p c f", c=2), y_ps,
                                              boB.rearrange("p (c f) -> p c f", c=2), ALU.add)
                ins.then_inc(S["y_sum"], 1)
                dve.wait_ge(S["y_sum"], t + 1)
                link(nc.vector.scalar_tensor_tensor(out=yt[:, i], in0=yt[:, i], scalar=0.0, in1=xres[:, t],
                                                    op0=ALU.max, op1=ALU.add))
                for c in range(2):
                    ins = nc.vector.bn_stats(stats[:, c], yt[:, i, c * HALF:(c + 1) * HALF])
                link(ins)
                nc.vector.bn_aggr(mv[:, i], stats[:].rearrange("p c s -> p (c s)")).then_inc(S["stat_done"], 1)
                dve.wait_ge(S["std_done"], t + 1)
                link(nc.vector.reciprocal(rstd[:, i, 1:2], rstd[:, i, 0:1]))
                if t >= 2:
                    dve.wait_ge(out_stored[i], 16 * (t // 2))
                nc.vector.tensor_scalar(yo[:, i], yt[:, i], mv[:, i, 0:1], rstd[:, i, 1:2], ALU.subtract,
                                        ALU.mult).then_inc(S["yo_ready"], 1)

        @block.tensor
        def _(pe):
            mm = nc.tensor.matmul
            pe.wait_ge(S["consts_made"], 1)
            pe.wait_ge(S["edges_f"], 1)
            for which in range(2):
                for k in range(CK):
                    ins = nc.tensor.transpose(bank(which)[0:PT, k * CHUNKS:(k + 1) * CHUNKS], e_f[:, which, k],
                                              ident[0:CHUNKS, 0:CHUNKS])
                ins.then_inc(S["edgesT_ps"], 1)
            pe.wait_ge(S["reach_sb"], 1)
            for w in range(2):
                ins = nc.tensor.transpose(bank(2)[0:NT, w * 128:w * 128 + CHUNKS], reach[:, 2 + w],
                                          ident[0:CHUNKS, 0:CHUNKS])
            ins.then_inc(S["reachT_ps"], 1)
            pe.wait_ge(S["ab_sb"], 1)
            mm(bank(3)[0:1, 0:NT], ab[:, 0:1], ident[0:NT, 0:NT], start=True, stop=True)
            mm(bank(3)[0:1, NT:2 * NT], ab[:, 1:2], ident[0:NT, 0:NT], start=True, stop=True)
            mm(bank(3)[0:1, 2 * NT:3 * NT], ab[:, 2:3], before[:], start=True, stop=False)
            mm(bank(3)[0:1, 2 * NT:3 * NT], ab[:, 0:1], ident[0:NT, 0:NT], start=False, stop=True).then_inc(S["rows_ps"], 1)
            pe.wait_ge(S["table_sb"], 1)
            pe.wait_ge(S["edgesT_sb"], 2)

            pe.sem_inc(S["onehot_free"], CK * AHEAD + CK)
            pe.sem_inc(S["acc_free"], 2)
            with pe.Fori(0, NT // 2) as b2:
                for half in range(2):
                    b = 2 * b2 + half
                    acc = ps[0:PT, half * 3 * BANK:half * 3 * BANK + N]
                    first = pe.value_load(table[0:1, 0, ds(b, 1)], min_val=0, max_val=CHUNKS - 1)
                    end = pe.value_load(table[0:1, 1, ds(b, 1)], min_val=1, max_val=CHUNKS)
                    ahead = pe.value_load(table[0:1, 2, ds(b, 1)], min_val=SPARE, max_val=AHEAD + CHUNKS * NT)
                    pe.wait_ge(S["acc_free"], b + 1)
                    for o, w in COLS:
                        mm(acc[:, o:o + w], ident16, diag[:, ds((N - PT) - b * PT + o, w)], start=True, stop=False,
                           skip_group_check=True)
                    with pe.Fori(first, end) as c:
                        g = ahead + c
                        pe.wait_ge(S["dst_ready"], g + 1 + DSLOTS)
                        for k in range(CK):
                            pe.wait_ge(S["onehot_ready"], CK * g + k + 1)
                            for o, w in COLS:
                                ins = mm(acc[:, o:o + w],
                                         dst1h[:, ds(g % 2, 1), k, 0:PT].rearrange("p o n -> p (o n)"),
                                         src1h[:, k, o:o + w], start=False, stop=False, skip_group_check=True)
                            ins.then_inc(S["onehot_free"], 1)
                    for o, w in COLS:
                        ins = mm(acc[:, o:o + 2], zero16, diag[:, 0:2], start=False, stop=True,
                                 skip_group_check=True)
                    ins.then_inc(S["acc_ready"], 1)

            pe.wait_ge(S["x_in"], 16)
            pe.wait_ge(S["acc_free"], 2 + NT)
            for i in range(KT * len(GROUPS)):
                k, (g, w) = i // len(GROUPS), GROUPS[i % len(GROUPS)]
                if i >= 4:
                    pe.wait_ge(S["xT_odd" if i % 2 else "xT_even"], (i - 4) // 2 + 1)
                for t in range(w):
                    ins = nc.tensor.transpose(bank(4 + i % 4)[:, t * PT:(t + 1) * PT],
                                              xin[:, g + t, k * KP:(k + 1) * KP], ident[0:PT, 0:PT])
                ins.then_inc(S["xT_ps"], 1)
            pe.wait_ge(S["wah_in"], 16)
            pe.wait_ge(S["xT_even"], KT * len(GROUPS) // 2)
            pe.wait_ge(S["xT_odd"], KT * len(GROUPS) // 2)
            for m in range(KT):
                if m >= 2:
                    pe.wait_ge(S["x1_sb"], m - 1)
                for k in range(KT):
                    for o, w in COLS:
                        oo = (m % 2) * 3 * BANK + o
                        ins = mm(ps[:, oo:oo + w], W_ah_sb[:, k, m * KP:(m + 1) * KP], xT[:, k, o:o + w],
                                 start=(k == 0), stop=(k == KT - 1))
                    if k == KT - 1:
                        ins.then_inc(S["x1_ps"], 1)
                    step = KT * m + k
                    if step < NT * len(GROUPS):
                        j, (g, w) = step // len(GROUPS), GROUPS[step % len(GROUPS)]
                        if step >= 2:
                            pe.wait_ge(S["cntT_sb"], step - 1)
                        for t in range(w):
                            ins = nc.tensor.transpose(bank(6 + step % 2)[0:PT, t * PT:(t + 1) * PT],
                                                      cnt[:, g + t, j * PT:(j + 1) * PT], ident[0:PT, 0:PT])
                        ins.then_inc(S["cntT_ps"], 1)
            pe.wait_ge(S["x1_sb"], KT)
            pe.wait_ge(S["v_made"], 2 * HEADS * KT * LAYERS)
            for k in range(KT):
                for o, w in COLS:
                    ins = mm(ps[0:2 * LH, o:o + w], V[:, k], x1T[:, k, o:o + w], start=(k == 0), stop=(k == KT - 1))
            ins.then_inc(S["asadT_ps"], 1)
            pe.wait_ge(S["cntT_sb"], NT * len(GROUPS))
            pe.wait_ge(S["asadT_sb"], 1)
            for t in range(NT):
                ins = nc.tensor.transpose(bank(7)[0:PT, t * 2 * LH:(t + 1) * 2 * LH], asadT[:, t * PT:(t + 1) * PT],
                                          ident[0:2 * LH, 0:2 * LH])
            ins.then_inc(S["asad_ps"], 1)
            pe.sem_inc(S["h_sb"], 2)

            def h_layer(l, last):
                pe.wait_ge(S["w_in"], 16 * (l + 1))
                for t in range(NT):
                    pe.wait_ge(S["h_sb"], NT * l + t + 1)
                    for k in range(KT):
                        for c in range(2):
                            o = (t % 2 * 2 + c) * BANK
                            ins = mm(ps[0:PT, o:o + HALF].rearrange("p (o f) -> p o f", o=1), x1T[:, k, t * PT:(t + 1) * PT],
                                     W_sb[:, ds(l, 1), k, c * HALF:(c + 1) * HALF],
                                     start=(k == 0), stop=(k == KT - 1))
                    ins.then_inc(S["h_ps"], 1)
                    if last and t == U_AT:
                        pe.wait_ge(S["amax_done"], 1)
                        for i, (g, w) in enumerate(GROUPS):
                            for tt in range(w):
                                ins = nc.tensor.transpose(bank(5 + i)[0:2 * LH, tt * PT:(tt + 1) * PT], u[:, g + tt],
                                                          ident[0:PT, 0:PT])
                            ins.then_inc(S["uT_ps"], 1)

            with pe.Fori(0, LAYERS - 1) as l:
                h_layer(l, False)
            h_layer(LAYERS - 1, True)

            pe.wait_ge(S["uT_sb"], len(GROUPS))
            pe.wait_ge(S["h_sb"], 2 + LAYERS * NT)
            pe.sem_inc(S["p_used"], PSLOTS)
            pe.sem_inc(S["attT_ps"], 1)

            def tile(p, r):
                p, r = p + r // (2 * NT), r % (2 * NT)
                q, j = r // NT, r % NT
                if j == 0:
                    pe.wait_ge(hB_in[q], 16 * p + 16)
                pe.wait_ge(S["p_ready"], 2 * NT * p + r + 1)
                for t in range(NT):
                    if j == 0 and t % 2 == 0:
                        pe.wait_ge(S["out_evac"], NT * (2 * p + q) + t + 2)
                    o = t * 256
                    ins = mm(ps[0:PT, o:o + HW], prob[:, r % PSLOTS, t * PT:(t + 1) * PT], hB[:, q, j],
                             start=(j == 0 and t % 2 == 0), stop=(j == NT - 1), skip_group_check=True)
                ins.then_inc(S["p_used"], 1)

            def features(p, k):
                if k == 0:
                    pe.wait_ge(S["out_evac"], NT * (2 * p + 2) + NT)
                for i, (g, w) in enumerate(GROUPS):
                    if k > 0:
                        pe.wait_ge(S["attT_sb"], 9 * p + 3 * (k - 1) + i + 2)
                    else:
                        pe.wait_ge(S["attT_sb"], 9 * p + 1)
                    for t in range(w):
                        ins = nc.tensor.transpose(bank(5 + i)[:, t * PT:(t + 1) * PT],
                                                  att[:, g + t, k * KP:(k + 1) * KP], ident[0:PT, 0:PT])
                    ins.then_inc(S["attT_ps"], 1)

            def pair(p, last):
                for r in range(FEAT, 2 * NT if last else 2 * NT + FEAT):
                    tile(p, r)
                    if r >= 2 * NT + FEAT - PK:
                        features(p, r - (2 * NT + FEAT - PK))
                if last:
                    for k in range(PK):
                        features(p, k)

            for r in range(FEAT):
                tile(0, r)
            with pe.Fori(0, PAIRS - 1) as p:
                pair(p, False)
            pair(PAIRS - 1, True)

            pe.wait_ge(S["wo_in"], 16)
            for t in range(NT):
                pe.wait_ge(xsn_early[t % 3], 16 * (t // 3 + 1))
                if t >= 2:
                    pe.wait_ge(S["y_sum"], t - 1)
                for k in range(OK):
                    if k == OK - PK:
                        pe.wait_ge(xsn_late[t % 3], 16 * (t // 3 + 1))
                    for c in range(2):
                        o = (t % 2 * 2 + c) * BANK
                        ins = mm(ps[0:PT, o:o + HALF], xsn[t % 3][:, k], Wo_sb[:, k, c * HALF:(c + 1) * HALF],
                                 start=(k == 0), stop=(k == OK - 1))
                ins.then_inc(S["y_ps"], 1)


_OUT = (N, D)


def kernel(**inputs):
    import numpy as np
    import concourse.bacc as bacc
    from concourse.bass_utils import run_bass_kernel_spmd

    i = {k: np.asarray(v) for k, v in inputs.items()}
    p = "L0_gnn_"
    arrays = {
        "x": i["x"], "src": i["src"], "dst": i["dst"],
        "W_ah": i[p + "W_ah"],
        "b_ah": i[p + "b_ah"].reshape(KT, KP).T,
        "W_all": np.stack([i[f"{p}W{l}"] for l in range(LAYERS)]),
        "a_all": np.stack([np.stack([i[f"{p}a_src{l}"].reshape(D), i[f"{p}a_dst{l}"].reshape(D)])
                           for l in range(LAYERS)]),
        "b_all": np.stack([i[f"{p}b{l}"] for l in range(LAYERS)]).reshape(OK, KP).T,
        "W_out": i[p + "W_out"],
        "b_out": i[p + "b_out"].reshape(1, D),
    }
    arrays = {f"in_{k}": np.ascontiguousarray(v) for k, v in arrays.items()}
    nc = bacc.Bacc("TRN2", target_bir_lowering=False, num_devices=1)
    args = [nc.dram_tensor(k, v.shape, mybir.dt.from_np(v.dtype), kind="ExternalInput").ap()
            for k, v in arrays.items()]
    args.append(nc.dram_tensor("out_0", _OUT, mybir.dt.float32, kind="ExternalOutput").ap())
    gnn_program(nc, *args)
    r = run_bass_kernel_spmd(nc, [arrays], core_ids=[0])
    return r.results[0]["out_0"]
```

```python
from contextlib import ExitStack

import concourse.bass as bass
from concourse import mybir

N, D = 1250, 768
LAYERS, HEADS = 3, 4
C = D // HEADS
EDGES = 41250
SLOPE = 0.2
EPS = 1e-05

PT = 125
NT = N // PT
KP = 128
KT = D // KP
LH = LAYERS * HEADS
CK = 3
CHUNKS = EDGES // (PT * CK)
FIELD = 7
DSLOTS = 4
SPARE = 8
AHEAD = CHUNKS + SPARE
BANK = 512
COLS = [(c, min(BANK, N - c)) for c in range(0, N, BANK)]
GROUPS = [(g, min(4, NT - g)) for g in range(0, NT, 4)]
HALF = D // 2
HW = C + 1
PAIRS = LH // 2
DEFER = LH - 2
TAKEN = 2 * NT // (PAIRS - 2)
LATE_AT = (5, 14, 16, 18, 20)
PARTS = 2 * LAYERS
HI_FIRST = 3
HEAD_START = 3
FEAT = 6
EARLY = 2
U_AT = 3
PK = 2 * C // KP
OK = LAYERS * KT
PSLOTS = 5
XSLOTS = 2
VSLOTS = 5
NOBODY = -3.0e38
HUGE = 1.0e30


def gnn_program(nc, x, src, dst, W_ah, b_ah, W_all, a_all, b_all, W_out, b_out, out):
    f32, f32r, f16, bf16, i32 = mybir.dt.float32, mybir.dt.float32r, mybir.dt.float16, mybir.dt.bfloat16, mybir.dt.int32
    ALU, ACT, AX = mybir.AluOpType, mybir.ActivationFunctionType, mybir.AxisListType
    ds = bass.ds

    h_dram = nc.dram_tensor("h_dram", (N, LH, C), f32).ap()
    as_dram = nc.dram_tensor("as_dram", (LH, N), f32).ap()
    u_dram = nc.dram_tensor("u_dram", (2 * LH, N), f32).ap()
    xs_dram = nc.dram_tensor("xs_dram", (NT, KP, OK, PT), f32).ap()

    with ExitStack() as ctx:
        def sb(name, shape, dt=f32):
            return ctx.enter_context(nc.sbuf_tensor(name, shape, dt))

        def sem(name):
            return ctx.enter_context(nc.semaphore(name))

        at = {}

        def region(name, words):
            at[name] = -(-nc.sbuf_base // 32) * 32
            return sb(name, [128, words])

        R_CNT = region("R_CNT", NT * N + 4)
        R_CNTT = region("R_CNTT", NT * N + 4)
        R_SMALL = region("R_SMALL", 4072)
        R_HOUT = region("R_HOUT", 2 * D)
        R_X1 = region("R_X1", 7592)
        R_W = region("R_W", OK * D)
        assert at["R_SMALL"] == at["R_CNTT"] + 4 * (NT * N + 4)

        def up8(words):
            return -(-words // 8) * 8

        def rounded(name, region, start, shape):
            return nc.alloc_sbuf_tensor_at(name, [128, *shape], f32r, offset=at[region] + 4 * start)

        def view(region, start, rows, shape, dt=f32):
            size = 1
            for s in shape:
                size *= s
            words = size * (2 if dt in (f16, bf16) else 4) // 4
            v = region[0:rows, start:start + words]
            if dt != f32:
                v = v.bitcast(dt)
            names = "abcd"[:len(shape)]
            if len(shape) > 1:
                v = v.rearrange(f"p ({' '.join(names)}) -> p {' '.join(names)}",
                                **dict(zip(names[1:], shape[1:])))
            return v, start + words

        cnt, _ = view(R_CNT, 0, PT, (NT, N))
        cntT, _ = view(R_CNTT, 0, PT, (NT, N))
        e_int, o = view(R_X1, 0, CHUNKS, (2, CK, PT), i32)
        e_f, o = view(R_X1, o, CHUNKS, (2, CK, PT))
        edgeT, o = view(R_X1, o, PT, (2, CK, (1 << FIELD) + 2))
        span, o = view(R_X1, o, CHUNKS, (2,))
        reach, o = view(R_X1, o, CHUNKS, (4, NT))
        blkpos, o = view(R_X1, o, CHUNKS, (2, NT))
        chunkno, o_dist = view(R_X1, o, CHUNKS, (2,))
        x1T, _ = view(R_X1, 0, KP, (KT, N))
        xin, _ = view(R_CNTT, 0, PT, (NT, D))
        Wv, o = view(R_SMALL, 0, KP, (VSLOTS, D))
        Wa, _ = view(R_SMALL, o, KP, (2, C), bf16)
        W_ah_sb, o = view(R_W, 0, KP, (KT, D))
        xT, _ = view(R_W, o, KP, (KT, N))
        Wo_sb, _ = view(R_W, 0, KP, (OK, D))
        src1h, o = view(R_SMALL, 0, PT, (CK, N), f16)
        dst1h, o = view(R_SMALL, o, PT, (2, CK, 128), f16)
        diag, o = view(R_SMALL, o, PT, (2 * N - PT + 1,), f16)
        nodes, _ = view(R_SMALL, o, PT, (N,), f16)
        dist, _ = view(R_X1, o_dist, PT, (DSLOTS, CK, PT))
        mask, o = view(R_W, 0, PT, (NT, N), bf16)
        asB, o_slot = view(R_W, o, PT, (2, N))
        masked, _ = view(R_SMALL, KT * HALF, PT, (2, N), bf16)
        z, _ = view(R_SMALL, KT * HALF + N, PT, (2, NT, LH))
        uT, _ = view(R_SMALL, KT * HALF, 2 * LH, (N,))
        x1_hi = rounded("x1_hi", "R_CNT", 0, (KT, N))
        x1_lo = rounded("x1_lo", "R_X1", 0, (KT, N))
        w_raw, _ = view(R_SMALL, 0, KP, (KT, HALF))
        wb = up8(o_slot)
        Wl_hi = [rounded("Wl_hi0", "R_CNT", up8(KT * N), (KT, HALF)), rounded("Wl_hi1", "R_W", wb, (KT, HALF))]
        Wl_lo = [rounded("Wl_lo0", "R_CNT", up8(KT * N) + KT * HALF, (KT, HALF)),
                 rounded("Wl_lo1", "R_W", wb + KT * HALF, (KT, HALF))]
        uB1, o = view(R_CNT, 0, PT, (2, N))
        prob4, o = view(R_CNT, o, PT, (PSLOTS - 1, N))
        prob = [prob4[:, i] for i in range(PSLOTS - 1)] + [view(R_HOUT, 0, PT, (N,))[0]]
        uB0, o = view(R_CNT, o, PT, (2, N))
        uB = [uB0, uB1]
        expo, _ = view(R_CNT, o, PT, (XSLOTS, N))
        hB, _ = view(R_SMALL, 0, PT, (2, NT, HW))
        masked2, o2 = view(R_W, o_slot, PT, (TAKEN, N), bf16)
        z2, o2 = view(R_W, o2, PT, (2, NT, LH))
        amax_late, _ = view(R_W, o2 + N, PT, (NT,))
        uT2, _ = view(R_W, o2, 2 * LH, (N,))
        att, o = view(R_X1, 0, PT, (NT, 2 * C))
        xsT, _ = view(R_X1, o, KP, (PK, N))
        Wo_hi = rounded("Wo_hi", "R_CNTT", 0, (OK, D))
        Wo_lo = rounded("Wo_lo", "R_W", 0, (OK, D))
        xs_first, _ = view(R_CNT, KT * N, KP, (OK, PT))
        xs_raw = [view(R_CNT, KT * N + OK * PT, KP, (OK, PT))[0], view(R_CNT, 0, KP, (OK, PT))[0]]
        xs_hi = [rounded("xs_hi0", "R_X1", 0, (OK, PT)), rounded("xs_hi1", "R_CNT", up8(2 * N), (OK, PT))]
        xs_lo = [rounded("xs_lo0", "R_X1", up8(OK * PT), (OK, PT)), rounded("xs_lo1", "R_CNT", up8(2 * N) + up8(OK * PT), (OK, PT))]
        early = OK - PK
        xres, _ = view(R_HOUT, 0, PT, (2, D))
        yt, o = view(R_SMALL, OK * D - NT * N - 4, PT, (2, D))
        boB, _ = view(R_SMALL, o, PT, (D,))
        yo, _ = view(R_X1, 2 * up8(OK * PT), PT, (2, D))

        h_outs, _ = view(R_HOUT, 0, 128, (2, D))
        h_out = h_outs[0:PT]
        aB = h_outs
        ident = sb("ident", [128, 128])
        ident16 = diag[:, N - PT:N]
        zero16 = diag[:, 0:PT]
        before = sb("before", [NT, NT])
        u_place = sb("u_place", [128, NT * 2 * LH])
        u = u_place[0:PT].rearrange("p (t h) -> p t h", t=NT)
        V = u_place[:, 0:KT * 2 * LH].rearrange("p (k h) -> p k h", k=KT)
        asad = sb("asad", [PT, NT, 2 * LH])
        s08 = sb("s08", [PT, NT, LH])
        s02 = sb("s02", [PT, NT, LH])
        amax = sb("amax", [PT, NT, LH])
        asadT = h_outs[0:2 * LH].rearrange("p a f -> p (a f)")[:, 0:N]
        b_ah_sb = sb("b_ah_sb", [KP, KT])
        b_all_sb = sb("b_all_sb", [KP, OK])
        b_pair = sb("b_pair", [KP, PK])
        rsum = sb("rsum", [PT, 2, NT])
        rinv = sb("rinv", [PT, 2, NT])
        ab = sb("ab", [NT, 3])
        row = sb("row", [1, 3, NT], i32)
        table = sb("table", [1, NT], i32)
        stats = sb("stats", [PT, 2, 6])
        mv = sb("mv", [PT, 2, 2])
        rstd = sb("rstd", [PT, 2, 2])
        epsc = sb("epsc", [PT, 1])

        ps = ctx.enter_context(nc.psum_tensor("ps", [128, 8 * BANK], f32))
        bank = lambda b: ps[:, b * BANK:(b + 1) * BANK]

        def out_at(q, t):
            return t * 256 + (3 * BANK if q == 1 and t >= 4 else 0)

        OWN_FIRST = list(range(4, NT)) + list(range(4))

        names = """edges_in x_in wah_in small_in consts_made edges_f edgesT_ps edgesT_sb reach_sb reachT_ps
            ab_sb rows_ps table_sb xT_ps xT_even xT_odd dst_ready dist_done onehot_ready onehot_free acc_ready acc_free
            v_made x1_ps x1_sb asad_ps asadT_sb as_stored
            cntT_ps cntT_sb masked_done max_made mask_ready scores_ready b_pair_sb uT_ps uT_sb u_stored
            x1_hi x1_lo x1_used late_as_in late_moved w_in w_hi w_lo h_ps h_sb x_ready exp_done p_ready p_used hB_ones
            rsum_sb rinv_sb out_evac attT_ps attT_sb xs_stored xs_free u_used wo_in
            first_in late_hi late_lo bo_in wo_hi wo_used wo_lo xs_hi xs_lo res_used y_ps y_sum stat_done std_done yo_ready chain pchain amax_done""".split()
        S = {n: sem(n) for n in names}
        asB_in = [sem("asB_in0"), sem("asB_in1")]
        h_stored = [sem("h_stored0"), sem("h_stored1")]
        uB_in = [sem("uB_in0"), sem("uB_in1")]
        hB_in = [sem("hB_in0"), sem("hB_in1")]
        xs_in = [sem("xs_in0"), sem("xs_in1")]
        res_in = [sem("res_in0"), sem("res_in1")]
        a_in = [sem(f"a_in{l}") for l in range(LAYERS)]
        wv_in = [sem(f"wv_in{i}") for i in range(VSLOTS)]
        out_stored = [sem("out_stored0"), sem("out_stored1")]

        block = ctx.enter_context(nc.Block())

        def chunks_of(eng, b):
            v = eng.value_load(table[0:1, ds(b, 1)], min_val=SPARE << 2 * FIELD,
                               max_val=(AHEAD + CHUNKS * NT + 1 << 2 * FIELD) - 1)
            n = 1 << FIELD
            return eng.snap(v % n), eng.snap(v // n % n), eng.snap(v // (n * n))

        @block.sync
        def _(sp):
            sp.dma_start(e_int[:, 0], dst.rearrange("(c k e) -> c k e", k=CK, e=PT)).then_inc(S["edges_in"], 16)
            sp.dma_start(e_int[:, 1], src.rearrange("(c k e) -> c k e", k=CK, e=PT)).then_inc(S["edges_in"], 16)
            sp.dma_start(xin, x.rearrange("(t p) f -> p t f", p=PT)).then_inc(S["x_in"], 16)
            sp.dma_start(W_ah_sb, W_ah.rearrange("(k p) f -> p k f", p=KP)).then_inc(S["wah_in"], 16)
            sp.dma_start(b_ah_sb[:], b_ah).then_inc(S["small_in"], 16)
            sp.dma_start(b_all_sb[:], b_all).then_inc(S["small_in"], 16)

            sp.wait_ge(S["acc_ready"], NT)
            for l in range(LAYERS):
                if l > 0:
                    sp.wait_ge(S["v_made"], 2 * HEADS * KT * l)
                sp.dma_start(aB.rearrange("p w f -> p (w f)"),
                             a_all[l:l + 1].rearrange("l w f -> l (w f)").broadcast_to((KP, 2 * D))).then_inc(a_in[l], 16)
                for k in range(KT):
                    i = KT * l + k
                    if i >= VSLOTS:
                        sp.wait_ge(S["v_made"], 2 * HEADS * (i - VSLOTS + 1))
                    sp.dma_start(Wv[:, i % VSLOTS], W_all[l, k * KP:(k + 1) * KP]).then_inc(wv_in[i % VSLOTS], 16)

            def load_w(n):
                if n > 0:
                    sp.wait_ge(S["w_lo"], n)
                sp.dma_start(w_raw, W_all[n // 2].rearrange("(k p) f -> p k f", p=KP)
                             [:, :, n % 2 * HALF:(n % 2 + 1) * HALF]).then_inc(S["w_in"], 16)

            def load_as(hh):
                if hh >= 2:
                    sp.wait_ge(S["max_made"], NT * (hh - 1))
                sp.dma_start(asB[:, hh % 2], as_dram[hh:hh + 1].broadcast_to((PT, N))).then_inc(asB_in[hh % 2], 16)

            def load_late_as(p):
                sp.dma_start(asB[:, 0], as_dram[ds(DEFER + p // 2, 1)].broadcast_to((PT, N))).then_inc(S["late_as_in"], 16)

            sp.wait_ge(S["v_made"], 2 * HEADS * KT * LAYERS)
            load_w(0)
            sp.wait_ge(S["x1_ps"], KT)
            sp.wait_ge(S["asadT_sb"], 1)
            sp.dma_start(as_dram, asadT[0:LH]).then_inc(S["as_stored"], 16)
            load_w(1)
            sp.wait_ge(S["as_stored"], 16)
            load_as(0)
            load_as(1)
            load_w(2)
            for hh in range(2, DEFER):
                load_as(hh)
                if hh % 2 and 2 + hh // 2 < PARTS:
                    load_w(2 + hh // 2)

            sp.wait_ge(S["uT_sb"], len(GROUPS))
            sp.dma_start(u_dram, uT).then_inc(S["u_stored"], 16)
            sp.wait_ge(S["u_stored"], 16)
            uu = u_dram.rearrange("(w h) n -> h w n", w=2)

            def load_u(p, q):
                sp.dma_start(uB[q], uu[ds(2 * p + q, 1)].broadcast_to((PT, 2, N))).then_inc(uB_in[q], 16)

            def load_h(p, q):
                sp.dma_start(hB[:, q, :, 0:C].rearrange("n t (o c) -> n t o c", o=1), h_dram.rearrange("(t n) h c -> n t h c", n=PT)[:, :, ds(2 * p + q, 1)]
                             ).then_inc(hB_in[q], 16)

            sp.wait_ge(S["h_ps"], NT * (PARTS - 1))
            load_u(0, 0)
            load_late_as(0)
            sp.wait_ge(h_stored[0], 16 * (NT // 2 + 1))
            sp.wait_ge(h_stored[1], 16 * (NT // 2 + 1))
            sp.wait_ge(S["hB_ones"], 1)
            for q in range(2):
                load_h(0, q)
            sp.wait_ge(S["h_ps"], NT * PARTS)
            load_u(0, 1)
            sp.wait_ge(h_stored[0], 16 * (LAYERS * NT // 2 + 1))
            sp.wait_ge(h_stored[1], 16 * (LAYERS * NT // 2 + 1))

            def load_pair(p):
                for q in range(2):
                    sp.wait_ge(S["u_used"], 2 * p + q - 1)
                    load_u(p, q)
                    sp.wait_ge(S["p_used"], PSLOTS + NT * (2 * p + q - 1))
                    load_h(p, q)

            with sp.Fori(1, PAIRS - 2) as p:
                load_pair(p)
                sp.wait_ge(S["max_made"], NT * DEFER + TAKEN * p)
                load_late_as(p)
            load_pair(PAIRS - 2)
            sp.wait_ge(S["uT_sb"], 2 * len(GROUPS))
            for w in range(2):
                rows = slice(w * LH + DEFER, (w + 1) * LH)
                sp.dma_start(u_dram[rows], uT2[rows]).then_inc(S["u_stored"], 16)
            sp.wait_ge(S["u_stored"], 16 * 3)
            load_pair(PAIRS - 1)

            sp.wait_ge(S["xs_stored"], 16 * PK * (PAIRS - 1))
            sp.wait_ge(S["u_used"], LH - 1)
            sp.dma_start(xs_first[:, 0:early], xs_dram[0, :, 0:early]).then_inc(S["first_in"], 16)

            sp.wait_ge(S["u_used"], LH)
            sp.dma_start(xs_raw[1][:, 0:early], xs_dram[1, :, 0:early]).then_inc(xs_in[1], 16)

            def load_xs(t):
                if t >= 3:
                    sp.wait_ge(S["xs_hi"], t - 2)
                    sp.wait_ge(S["xs_lo"], t - 2)
                sp.dma_start(xs_raw[t % 2], xs_dram[t]).then_inc(xs_in[t % 2], 16)

            def load_res(t):
                if t >= 2:
                    sp.wait_ge(S["res_used"], t - 1)
                sp.dma_start(xres[:, t % 2], x[t * PT:(t + 1) * PT]).then_inc(res_in[t % 2], 16)

            def store(t):
                sp.wait_ge(S["yo_ready"], t + 1)
                sp.dma_start(out[t * PT:(t + 1) * PT], yo[:, t % 2]).then_inc(out_stored[t % 2], 16)

            sp.wait_ge(S["p_used"], PSLOTS + LH * NT)
            for t in range(2):
                load_res(t)
            sp.dma_start(boB, b_out.broadcast_to((PT, D))).then_inc(S["bo_in"], 16)
            sp.wait_ge(S["xs_stored"], 16 * PK * PAIRS)
            load_xs(2)
            for t in range(3, NT):
                load_xs(t)
                load_res(t - 1)
                store(t - 3)
            load_res(NT - 1)
            for t in range(NT - 3, NT):
                store(t)
            sp.wait_ge(out_stored[0], 16 * (NT // 2))
            sp.wait_ge(out_stored[1], 16 * (NT // 2))

        @block.gpsimd
        def _(pool):
            n = [0]

            def link(ins):
                n[0] += 1
                ins.then_inc(S["pchain"], 1)
                pool.wait_ge(S["pchain"], n[0])

            link(nc.gpsimd.memset(ident[:], 0.0))
            link(nc.gpsimd.affine_select(out=ident[:], in_=ident[:], compare_op=ALU.not_equal, fill=1.0,
                                         base=0, pattern=[[-1, 128]], channel_multiplier=1))
            link(nc.gpsimd.memset(before[:], 1.0))
            link(nc.gpsimd.affine_select(out=before[:], in_=before[:], compare_op=ALU.is_gt, fill=0.0,
                                         base=0, pattern=[[1, NT]], channel_multiplier=-1))
            link(nc.gpsimd.memset(diag, 0.0))
            link(nc.gpsimd.tensor_copy(ident16, ident[0:PT, 0:PT]))
            link(nc.gpsimd.iota(nodes, pattern=[[1, N]], base=0, channel_multiplier=0,
                                allow_small_or_imprecise_dtypes=True))
            link(nc.gpsimd.iota(blkpos[:, 0], pattern=[[PT, NT]], base=0, channel_multiplier=0,
                                allow_small_or_imprecise_dtypes=True))
            link(nc.gpsimd.iota(blkpos[:, 1], pattern=[[PT, NT]], base=PT - 1, channel_multiplier=0,
                                allow_small_or_imprecise_dtypes=True))
            link(nc.gpsimd.iota(chunkno[:, 0:1], pattern=[[0, 1]], base=CHUNKS, channel_multiplier=-1,
                                allow_small_or_imprecise_dtypes=True))
            nc.gpsimd.iota(chunkno[:, 1:2], pattern=[[0, 1]], base=1, channel_multiplier=1,
                           allow_small_or_imprecise_dtypes=True).then_inc(S["consts_made"], 1)

            pool.wait_ge(S["u_stored"], 16)
            pool.wait_ge(S["w_lo"], PARTS)
            nc.gpsimd.memset(hB[:, :, :, C:HW], 1.0).then_inc(S["hB_ones"], 1)

            def store_pair(p):
                for k in range(PK):
                    pool.wait_ge(S["attT_sb"], 9 * p + 3 * k + 4)
                    pool.dma_start(xs_dram.rearrange("t p k n -> p k t n")[:, ds(PK * p + k, 1)],
                                   xsT[:, k].rearrange("p (o t n) -> p o t n", o=1, n=PT)).then_inc(S["xs_stored"], 16)
                pool.wait_ge(S["xs_stored"], 16 * PK * (p + 1))
                pool.sem_inc(S["xs_free"], 1)

            pool.sem_inc(S["xs_free"], 1)
            with pool.Fori(0, PAIRS - 2) as p:
                store_pair(p)
            pool.wait_ge(S["max_made"], LH * NT)
            pool.wait_ge(S["u_stored"], 16 * 3)
            pool.dma_start(Wo_sb, W_out.rearrange("(k p) f -> p k f", p=KP)).then_inc(S["wo_in"], 16)
            for p in range(PAIRS - 2, PAIRS):
                store_pair(p)

        @block.scalar
        def _(act):
            act.wait_ge(S["table_sb"], 1)
            act.wait_ge(S["edgesT_sb"], 2)
            act.sem_inc(S["dst_ready"], AHEAD + DSLOTS)

            def distances(b, c, g):
                act.wait_ge(S["dst_ready"], g + 1)
                act.wait_ge(S["edgesT_sb"], 2)
                for k in range(CK):
                    nc.scalar.activation(dist[:, ds(g % DSLOTS, 1), k], nodes[:, ds(b * PT, PT)].rearrange("p (o n) -> p o n", o=1),
                                         ACT.Abs, bias=edgeT[:, 0, k, ds(c, 1)], scale=-1.0).then_inc(S["dist_done"], 1)

            def dst_onehots(b):
                first, end, ahead = chunks_of(act, b)
                act.wait_ge(S["dist_done"], CK * (ahead + first + b))
                distances(b, first, ahead + first)
                with act.Fori(first, end) as c:
                    g = ahead + c
                    distances(b, c + 1, g + 1)
                    act.wait_ge(S["dist_done"], CK * (g + b) + CK)
                    act.wait_ge(S["onehot_free"], CK * g)
                    act.wait_ge(S["edgesT_sb"], 2)
                    nc.scalar.activation(dst1h[:, ds(g % 2, 1), :, 0:PT].rearrange("p o k n -> p (o k) n"),
                                         dist[:, ds(g % DSLOTS, 1)].rearrange("p o k n -> p (o k) n"),
                                         ACT.Relu, bias=1.0, scale=-1.0).then_inc(S["dst_ready"], 1)

            def counts_out(b2, half):
                act.wait_ge(S["acc_ready"], 2 * b2 + half + 1)
                nc.scalar.copy(cnt[:, ds(2 * b2 + half, 1)],
                               ps[0:PT, half * 3 * BANK:half * 3 * BANK + N].rearrange("p (o n) -> p o n", o=1)
                               ).then_inc(S["acc_free"], 1)

            act.sem_inc(S["dist_done"], CK * AHEAD)
            dst_onehots(0)
            with act.Fori(0, NT // 2 - 1) as b2:
                for half in range(2):
                    dst_onehots(2 * b2 + half + 1)
                    counts_out(b2, half)
            dst_onehots(NT - 1)
            for half in range(2):
                counts_out(NT // 2 - 1, half)
            for i in range(0, KT * len(GROUPS), 2):
                k, (g, w) = i // len(GROUPS), GROUPS[i % len(GROUPS)]
                act.wait_ge(S["xT_ps"], i + 1)
                nc.scalar.copy(xT[:, k, g * PT:(g + w) * PT], bank(4 + i % 4)[:, 0:w * PT]).then_inc(S["xT_even"], 1)
            act.wait_ge(S["small_in"], 32)
            for step in range(KT * KT):
                if step < NT * len(GROUPS):
                    j, (g, w) = step // len(GROUPS), GROUPS[step % len(GROUPS)]
                    act.wait_ge(S["cntT_ps"], step + 1)
                    nc.scalar.copy(cntT[:, j, g * PT:(g + w) * PT], bank(6 + step % 2)[0:PT, 0:w * PT]
                                   ).then_inc(S["cntT_sb"], 1)
                if step % KT == KT - 1:
                    m = step // KT
                    act.wait_ge(S["x1_ps"], m + 1)
                    o = (m % 2) * 3 * BANK
                    nc.scalar.activation(x1T[:, m], ps[:, o:o + N], ACT.Relu, bias=b_ah_sb[:, m:m + 1]
                                         ).then_inc(S["x1_sb"], 1)
            def round_w(n, slot):
                act.wait_ge(S["w_in"], 16 * n + 16)
                nc.scalar.copy(Wl_hi[slot][:], w_raw).then_inc(S["w_hi"], 1)

            act.wait_ge(S["mask_ready"], NT - KT)
            round_w(0, 0)
            act.wait_ge(S["x1_sb"], KT)
            for m in range(KT):
                act.wait_ge(S["mask_ready"], NT - KT + m + 1)
                nc.scalar.copy(x1_hi[:, m], x1T[:, m]).then_inc(S["x1_hi"], 1)
            act.wait_ge(S["v_made"], 2 * HEADS * KT * LAYERS)
            act.wait_ge(S["x1_used"], KT)
            nc.scalar.copy(asadT, ps[0:2 * LH, 0:N]).then_inc(S["asadT_sb"], 1)
            act.wait_ge(S["as_stored"], 16)
            act.wait_ge(S["asad_ps"], 1)
            act.sem_inc(h_stored[0], 16)
            act.sem_inc(h_stored[1], 16)

            def shifts_out(first, place):
                for i, (g, w) in enumerate(GROUPS):
                    act.wait_ge(S["uT_ps"], first + i + 1)
                    nc.scalar.copy(place[:, g * PT:(g + w) * PT], bank(5 + i)[0:2 * LH, 0:w * PT]).then_inc(S["uT_sb"], 1)

            def h_part(l, c, last):
                for t in range(NT):
                    i, slot = 5 * c + t // 2, (5 * c + t // 2) % 2
                    act.wait_ge(S["h_ps"], NT * (2 * l + c) + t + 1)
                    if t % 2 == 0:
                        act.wait_ge(h_stored[slot], 16 * (NT // 2 * l + i // 2 + 1))
                    nc.scalar.copy(h_out[:, slot, t % 2 * HALF:(t % 2 + 1) * HALF],
                                   bank((2 * c + t) % 4)[0:PT, 0:HALF]).then_inc(S["h_sb"], 1)
                    if t % 2:
                        act.wait_ge(S["h_sb"], NT * (2 * l + c) + t + 5)
                        act.dma_start(h_dram.rearrange("(t p) (m h) c -> p t m (h c)", p=PT, h=2)
                                      [:, t - 1:t + 1, ds(2 * l + c, 1)],
                                      h_out[:, slot].rearrange("p (t o f) -> p t o f", t=2, o=1)
                                      ).then_inc(h_stored[slot], 16)
                    if t == 0 and not (last and c == 1):
                        round_w(2 * l + c + 1, 1 - c)
                    if t == U_AT and last and c == 1:
                        shifts_out(0, uT)

            def exp_tile(p, r):
                p, r = p + r // (2 * NT), r % (2 * NT)
                n = 2 * NT * p + r
                act.wait_ge(S["x_ready"], n + 1)
                act.wait_ge(S["p_used"], n + 1)
                act.wait_ge(S["scores_ready"], 1)
                nc.scalar.activation(prob[r % PSLOTS], expo[:, r % XSLOTS], ACT.Exp,
                                     bias=s02[:, r % NT, ds(2 * p + r // NT, 1)]).then_inc(S["exp_done"], 1)

            act.sem_inc(S["exp_done"], XSLOTS)
            act.sem_inc(S["out_evac"], NT + 1)
            act.sem_inc(S["attT_sb"], 1)
            with act.Fori(0, LAYERS - 1) as l:
                for c in range(2):
                    h_part(l, c, False)
            for c in range(2):
                h_part(LAYERS - 1, c, True)

            def head_out(p, q):
                act.wait_ge(S["rinv_sb"], 2 * p + q + 1)
                if q == 0:
                    act.wait_ge(S["attT_ps"], 9 * p + 1)
                for t in range(NT):
                    o = out_at(q, t)
                    nc.scalar.activation(att[:, t, q * C:(q + 1) * C], ps[0:PT, o:o + C], ACT.Copy,
                                         scale=rinv[:, q, t:t + 1]).then_inc(S["out_evac"], 1)

            def features(p, k):
                if k == 0:
                    act.wait_ge(S["xs_free"], p + 1)
                    nc.scalar.copy(b_pair[:], b_all_sb[:, ds(PK * p, PK)]).then_inc(S["b_pair_sb"], 1)
                    act.wait_ge(S["b_pair_sb"], p + 1)
                for i, (g, w) in enumerate(GROUPS):
                    act.wait_ge(S["attT_ps"], 9 * p + 3 * k + i + 2)
                    nc.scalar.activation(xsT[:, k, g * PT:(g + w) * PT], bank(5 + i)[:, 0:w * PT], ACT.Relu,
                                         bias=b_pair[:, k:k + 1]).then_inc(S["attT_sb"], 1)

            def pair(p, last, shifts_here=False):
                for r in range(NT, 2 * NT if last else 3 * NT):
                    exp_tile(p, r)
                    if shifts_here and r == NT:
                        shifts_out(len(GROUPS), uT2)
                    if r == NT + EARLY + XSLOTS:
                        head_out(p, 0)
                    if r == 2 * NT + EARLY + XSLOTS:
                        head_out(p, 1)
                    if not last and r >= 3 * NT - PK:
                        features(p, r - (3 * NT - PK))
                if last:
                    act.wait_ge(S["p_ready"], LH * NT)
                    act.wait_ge(S["wo_in"], 16)
                    for k in range(HI_FIRST):
                        round_wo(k)
                    head_out(p, 1)
                    for k in range(PK):
                        features(p, k)

            def round_wo(k):
                nc.scalar.copy(Wo_hi[:, k], Wo_sb[:, k]).then_inc(S["wo_hi"], 1)

            for r in range(NT):
                if r == PSLOTS - 1:
                    for slot in range(2):
                        act.wait_ge(h_stored[slot], 16 * (LAYERS * NT // 2 + 1))
                exp_tile(0, r)
            with act.Fori(0, PAIRS - 2) as p:
                pair(p, False)
            pair(PAIRS - 2, False, shifts_here=True)
            pair(PAIRS - 1, True)

            act.wait_ge(xs_in[1], 16)
            act.wait_ge(S["p_used"], PSLOTS + LH * NT)
            nc.scalar.copy(xs_hi[1][:, 0:early], xs_raw[1][:, 0:early]).then_inc(S["xs_hi"], 1)
            act.wait_ge(S["attT_sb"], 9 * PAIRS + 1)
            nc.scalar.copy(xs_hi[1][:, early:OK], xsT[:, :, PT:2 * PT]).then_inc(S["late_hi"], 1)
            for k in range(HI_FIRST, OK):
                round_wo(k)
            for t in range(NT):
                if 2 <= t + 1 < NT:
                    act.wait_ge(S["y_ps"], t)
                    if t == 1:
                        act.wait_ge(S["late_lo"], 1)
                    act.wait_ge(xs_in[(t + 1) % 2], 16 * ((t + 2) // 2 if t % 2 == 0 else (t + 1) // 2))
                    nc.scalar.copy(xs_hi[(t + 1) % 2][:], xs_raw[(t + 1) % 2]).then_inc(S["xs_hi"], 1)
                act.wait_ge(S["stat_done"], t + 1)
                nc.scalar.activation(rstd[:, t % 2, 0:1], mv[:, t % 2, 1:2], ACT.Sqrt, bias=epsc[:, 0:1]).then_inc(S["std_done"], 1)

        @block.vector
        def _(dve):
            n = [0]

            def link(ins):
                n[0] += 1
                ins.then_inc(S["chain"], 1)
                dve.wait_ge(S["chain"], n[0])

            nc.vector.memset(epsc[:], EPS)
            dve.wait_ge(S["edges_in"], 32)
            link(nc.vector.tensor_copy(e_f[:, 0], e_int[:, 0]))
            nc.vector.tensor_copy(e_f[:, 1], e_int[:, 1]).then_inc(S["edges_f"], 1)
            link(nc.vector.tensor_reduce(span[:, 0:1], e_f[:, 0], axis=AX.XY, op=ALU.min))
            link(nc.vector.tensor_reduce(span[:, 1:2], e_f[:, 0], axis=AX.XY, op=ALU.max))
            dve.wait_ge(S["consts_made"], 1)
            link(nc.vector.tensor_scalar(reach[:, 0], blkpos[:, 1], span[:, 0:1], None, ALU.is_ge))
            link(nc.vector.tensor_scalar(reach[:, 1], blkpos[:, 0], span[:, 1:2], None, ALU.is_le))
            link(nc.vector.tensor_tensor(reach[:, 0], reach[:, 0], reach[:, 1], ALU.mult))
            link(nc.vector.tensor_scalar(reach[:, 2], reach[:, 0], chunkno[:, 0:1], None, ALU.mult))
            nc.vector.tensor_scalar(reach[:, 3], reach[:, 0], chunkno[:, 1:2], None, ALU.mult).then_inc(S["reach_sb"], 1)
            nc.vector.memset(edgeT[:, 0, :, CHUNKS:CHUNKS + 2], -1.0)
            for which in range(2):
                dve.wait_ge(S["edgesT_ps"], which + 1)
                nc.vector.tensor_copy(edgeT[:, which, :, 0:CHUNKS], bank(which)[0:PT, 0:CK * CHUNKS]
                                      .rearrange("p (k c) -> p k c", k=CK)).then_inc(S["edgesT_sb"], 1)
            dve.wait_ge(S["reachT_ps"], 1)
            link(nc.vector.tensor_reduce(ab[:, 0:2], bank(2)[0:NT, 0:256].rearrange("p (w c) -> p w c", w=2)[:, :, 0:CHUNKS],
                                         axis=AX.X, op=ALU.max))
            link(nc.vector.tensor_scalar(ab[:, 0:1], ab[:, 0:1], 1.0, None, ALU.max))
            link(nc.vector.tensor_scalar(ab[:, 2:3], ab[:, 0:1], -1.0, CHUNKS + 1.0, ALU.mult, ALU.add))
            link(nc.vector.tensor_tensor(ab[:, 1:2], ab[:, 1:2], ab[:, 2:3], ALU.max))
            link(nc.vector.tensor_tensor(ab[:, 2:3], ab[:, 0:1], ab[:, 1:2], ALU.add))
            nc.vector.tensor_scalar(ab[:, 2:3], ab[:, 2:3], -float(CHUNKS), None, ALU.add).then_inc(S["ab_sb"], 1)
            dve.wait_ge(S["rows_ps"], 1)
            nc.vector.tensor_scalar(row[0:1, 0], bank(3)[0:1, 0:NT], -1.0, float(CHUNKS), ALU.mult, ALU.add)
            nc.vector.tensor_copy(row[0:1, 1], bank(3)[0:1, NT:2 * NT])
            link(nc.vector.tensor_scalar(row[0:1, 2], bank(3)[0:1, 2 * NT:3 * NT], float(SPARE), None, ALU.add))
            link(nc.vector.tensor_scalar(row[0:1, 1], row[0:1, 1], FIELD, None, ALU.logical_shift_left))
            link(nc.vector.tensor_scalar(row[0:1, 2], row[0:1, 2], 2 * FIELD, None, ALU.logical_shift_left))
            link(nc.vector.tensor_tensor(row[0:1, 0], row[0:1, 0], row[0:1, 1], ALU.bitwise_or))
            link(nc.vector.tensor_tensor(table[0:1], row[0:1, 0], row[0:1, 2], ALU.bitwise_or))
            dve.sem_inc(S["table_sb"], 1)

            dve.sem_inc(S["onehot_ready"], CK * AHEAD)
            with dve.Fori(0, NT) as b:
                first, end, ahead = chunks_of(dve, b)
                with dve.Fori(first, end) as c:
                    g = ahead + c
                    for k in range(CK):
                        dve.wait_ge(S["onehot_free"], CK * g + k + 1)
                        nc.vector.tensor_scalar(src1h[:, k], nodes, edgeT[:, 1, k, ds(c, 1)], None,
                                                ALU.is_equal).then_inc(S["onehot_ready"], 1)

            for i in range(1, KT * len(GROUPS), 2):
                k, (g, w) = i // len(GROUPS), GROUPS[i % len(GROUPS)]
                dve.wait_ge(S["xT_ps"], i + 1)
                nc.vector.tensor_copy(xT[:, k, g * PT:(g + w) * PT], bank(4 + i % 4)[:, 0:w * PT]).then_inc(S["xT_odd"], 1)
            for l in range(LAYERS):
                dve.wait_ge(a_in[l], 16)
                for k in range(KT):
                    i = KT * l + k
                    dve.wait_ge(wv_in[i % VSLOTS], 16 * (i // VSLOTS + 1))
                    for w in range(2):
                        for h in range(HEADS):
                            m = 2 * HEADS * i + HEADS * w + h
                            col = w * LH + l * HEADS + h
                            if m >= 2:
                                dve.wait_ge(S["v_made"], m - 1)
                            nc.vector.tensor_tensor_reduce(out=Wa[:, m % 2], in0=Wv[:, i % VSLOTS, h * C:(h + 1) * C],
                                                           in1=aB[:, w, h * C:(h + 1) * C], scale=1.0, scalar=0.0,
                                                           op0=ALU.mult, op1=ALU.add, accum_out=V[:, k, col:col + 1]
                                                           ).then_inc(S["v_made"], 1)
            dve.wait_ge(S["cntT_ps"], NT * len(GROUPS))
            dve.wait_ge(S["x1_ps"], KT)
            for b in list(range(KT, NT)) + list(range(KT)):
                nc.vector.tensor_scalar(mask[:, b], cnt[:, b], 0.0, NOBODY, ALU.is_equal, ALU.mult
                                        ).then_inc(S["mask_ready"], 1)

            def rest_w(n):
                dve.wait_ge(S["w_hi"], n + 1)
                nc.vector.tensor_tensor(Wl_lo[n % 2][:], w_raw, Wl_hi[n % 2][:].bitcast(f32), ALU.subtract
                                        ).then_inc(S["w_lo"], 1)

            rest_w(0)
            for m in range(KT):
                dve.wait_ge(S["x1_hi"], m + 1)
                dve.wait_ge(S["x1_used"], m + 1)
                nc.vector.tensor_tensor(x1_lo[:, m], x1T[:, m], x1_hi[:, m].bitcast(f32), ALU.subtract
                                        ).then_inc(S["x1_lo"], 1)
            dve.wait_ge(S["asad_ps"], 1)
            link(nc.vector.tensor_copy(asad[:], bank(7)[0:PT, 0:NT * 2 * LH].rearrange("p (t h) -> p t h", t=NT)))
            nc.vector.tensor_scalar(s08[:], asad[:, :, 0:LH], 1.0 - SLOPE, None, ALU.mult)
            link(nc.vector.tensor_scalar(s02[:], asad[:, :, 0:LH], SLOPE, None, ALU.mult))
            dve.sem_inc(S["scores_ready"], 1)
            dve.wait_ge(S["mask_ready"], NT)
            dve.wait_ge(S["v_made"], 2 * HEADS * KT * LAYERS)
            rest_w(1)
            for hh in range(DEFER):
                dve.wait_ge(asB_in[hh % 2], 16 * (hh // 2 + 1))
                if hh % 2 == 0 and 0 < hh // 2 < PARTS - 1:
                    rest_w(hh // 2 + 1)
                for b in range(NT):
                    i = NT * hh + b
                    if i >= 2:
                        dve.wait_ge(S["max_made"], i - 1)
                    nc.vector.tensor_tensor_reduce(out=masked[:, i % 2], in0=mask[:, b], in1=asB[:, hh % 2], scale=1.0,
                                                   scalar=NOBODY, op0=ALU.add, op1=ALU.max,
                                                   accum_out=amax[:, b, hh:hh + 1]).then_inc(S["max_made"], 1)

            def shifts(h0, h1, z):
                ad = asad[:, :, LH + h0:LH + h1]
                z0, z1 = z[:, 0, :, 0:h1 - h0], z[:, 1, :, 0:h1 - h0]
                dve.wait_ge(S["max_made"], NT * h1)
                link(nc.vector.tensor_tensor(z0, amax[:, :, h0:h1], ad, ALU.add))
                link(nc.vector.tensor_scalar(z1, z0, SLOPE, None, ALU.mult))
                link(nc.vector.tensor_tensor(z0, z0, z1, ALU.max))
                link(nc.vector.tensor_scalar(z1, ad, SLOPE, None, ALU.mult))
                link(nc.vector.tensor_tensor(u[:, :, h0:h1], ad, z0, ALU.subtract))
                link(nc.vector.tensor_tensor(u[:, :, LH + h0:LH + h1], z1, z0, ALU.subtract))
                dve.sem_inc(S["amax_done"], 1)

            for w in range(2):
                link(nc.vector.memset(u[:, :, w * LH + DEFER:(w + 1) * LH], 0.0))
            shifts(0, DEFER, z)

            def exponent_tile(p, r):
                p, r = p + r // (2 * NT), r % (2 * NT)
                n = 2 * NT * p + r
                q = r // NT
                if r % NT == 0:
                    dve.wait_ge(uB_in[q], 16 * p + 16)
                dve.wait_ge(S["exp_done"], n + 1)
                nc.vector.scalar_tensor_tensor(out=expo[:, r % XSLOTS], in0=uB[q][:, 0],
                                               scalar=s08[:, r % NT, ds(2 * p + q, 1)], in1=uB[q][:, 1],
                                               op0=ALU.add, op1=ALU.max).then_inc(S["x_ready"], 1)
                if r % NT == NT - 1:
                    dve.wait_ge(S["x_ready"], n + 1)
                    dve.sem_inc(S["u_used"], 1)

            def weight_tile(p, r):
                p, r = p + r // (2 * NT), r % (2 * NT)
                dve.wait_ge(S["exp_done"], 2 * NT * p + r + XSLOTS + 1)
                nc.vector.scalar_tensor_tensor(out=prob[r % PSLOTS], in0=prob[r % PSLOTS], scalar=HUGE,
                                               in1=cntT[:, r % NT], op0=ALU.min, op1=ALU.mult
                                               ).then_inc(S["p_ready"], 1)

            def invert(p, q):
                dve.wait_ge(S["p_used"], 2 * NT * p + NT * (q + 1) + PSLOTS)
                dve.wait_ge(S["out_evac"], NT * (2 * p + q + 1) + 1)
                for t0, t1 in ((0, 4), (4, NT)):
                    o = out_at(q, t0)
                    ins = nc.vector.tensor_scalar(rsum[:, q, t0:t1], ps[0:PT, o:o + (t1 - t0) * 256]
                                                  .rearrange("p (t w) -> p t w", w=256)[:, :, C], 1e-16, None, ALU.add)
                ins.then_inc(S["rsum_sb"], 1)
                dve.wait_ge(S["rsum_sb"], 2 * p + q + 1)
                nc.vector.reciprocal(rinv[:, q], rsum[:, q]).then_inc(S["rinv_sb"], 1)

            def late_ready(pp, e):
                dve.wait_ge(S["late_as_in"], 16 * (2 * pp + e) + 16)
                dve.wait_ge(S["late_moved"], pp + 1)
                dve.wait_ge(S["max_made"], NT * (DEFER + pp) + e * TAKEN)

            def late_max(pp, e, j):
                b = e * TAKEN + j
                nc.vector.tensor_tensor_reduce(out=masked2[:, j], in0=mask[:, b], in1=asB[:, 0], scale=1.0,
                                               scalar=NOBODY, op0=ALU.add, op1=ALU.max,
                                               accum_out=amax_late[:, b:b + 1]).then_inc(S["max_made"], 1)

            def late_move(pp):
                dve.wait_ge(S["max_made"], NT * (DEFER + pp) + NT)
                nc.vector.tensor_copy(amax[:, :, ds(DEFER + pp, 1)].rearrange("p t o -> p (t o)"), amax_late
                                      ).then_inc(S["late_moved"], 1)

            def pair(p, last, late=None):
                for r in range(EARLY + 1, (2 * NT if last else 2 * NT + EARLY + 1)):
                    if late is not None and r == EARLY + 1:
                        late_ready(*late)
                    if not (last and r + XSLOTS >= 2 * NT):
                        exponent_tile(p, r + XSLOTS)
                    weight_tile(p, r)
                    for j in range(TAKEN):
                        if late is not None and LATE_AT[j] == r:
                            late_max(*late, j)
                    if r == NT + EARLY:
                        invert(p, 0)
                invert(p, 1)
                if late is not None and late[1] == 1:
                    late_move(late[0])

            for r in range(XSLOTS):
                exponent_tile(0, r)
            for r in range(EARLY + 1):
                exponent_tile(0, r + XSLOTS)
                weight_tile(0, r)
            dve.wait_ge(S["h_ps"], NT * PARTS)
            dve.sem_inc(S["late_moved"], 1)
            with dve.Fori(0, (PAIRS - 2) // 2) as pp:
                for e in range(2):
                    pair(2 * pp + e, False, late=(pp, e))
            dve.wait_ge(S["late_moved"], 3)
            shifts(DEFER, LH, z2)
            pair(PAIRS - 2, False)
            pair(PAIRS - 1, True)

            def rest_wo(k):
                dve.wait_ge(S["wo_hi"], k + 1)
                dve.wait_ge(S["wo_used"], k + 1)
                nc.vector.tensor_tensor(Wo_lo[:, k], Wo_sb[:, k], Wo_hi[:, k].bitcast(f32), ALU.subtract
                                        ).then_inc(S["wo_lo"], 1)

            def rest_xs(t):
                dve.wait_ge(S["xs_hi"], t)
                nc.vector.tensor_tensor(xs_lo[t % 2][:], xs_raw[t % 2], xs_hi[t % 2][:].bitcast(f32), ALU.subtract
                                        ).then_inc(S["xs_lo"], 1)

            for k in range(HEAD_START):
                rest_wo(k)
            dve.wait_ge(S["xs_hi"], 1)
            nc.vector.tensor_tensor(xs_lo[1][:, 0:early], xs_raw[1][:, 0:early], xs_hi[1][:, 0:early].bitcast(f32),
                                    ALU.subtract).then_inc(S["xs_lo"], 1)
            dve.wait_ge(S["late_hi"], 1)
            nc.vector.tensor_tensor(xs_lo[1][:, early:OK], xsT[:, :, PT:2 * PT], xs_hi[1][:, early:OK].bitcast(f32),
                                    ALU.subtract).then_inc(S["late_lo"], 1)
            for k in range(HEAD_START, OK):
                rest_wo(k)
            dve.wait_ge(S["bo_in"], 16)
            dve.wait_ge(S["xs_stored"], 16 * PK * PAIRS)
            for t in range(NT):
                i = t % 2
                if 2 <= t + 1 < NT:
                    rest_xs(t + 1)
                dve.wait_ge(S["y_ps"], t + 1)
                y_ps = ps[0:PT, (1 - i) * 2 * BANK:(2 - i) * 2 * BANK].rearrange("p (c f) -> p c f", c=2)[:, :, 0:HALF]
                ins = nc.vector.tensor_tensor(yt[:, i].rearrange("p (c f) -> p c f", c=2), y_ps,
                                              boB.rearrange("p (c f) -> p c f", c=2), ALU.add)
                ins.then_inc(S["y_sum"], 1)
                dve.wait_ge(S["y_sum"], t + 1)
                dve.wait_ge(res_in[i], 16 * (t // 2 + 1))
                nc.vector.scalar_tensor_tensor(out=yt[:, i], in0=yt[:, i], scalar=0.0, in1=xres[:, i],
                                               op0=ALU.max, op1=ALU.add).then_inc(S["res_used"], 1)
                dve.wait_ge(S["res_used"], t + 1)
                for c in range(2):
                    ins = nc.vector.bn_stats(stats[:, c], yt[:, i, c * HALF:(c + 1) * HALF])
                link(ins)
                nc.vector.bn_aggr(mv[:, i], stats[:].rearrange("p c s -> p (c s)")).then_inc(S["stat_done"], 1)
                dve.wait_ge(S["std_done"], t + 1)
                link(nc.vector.reciprocal(rstd[:, i, 1:2], rstd[:, i, 0:1]))
                if t >= 2:
                    dve.wait_ge(out_stored[i], 16 * (t // 2))
                nc.vector.tensor_scalar(yo[:, i], yt[:, i], mv[:, i, 0:1], rstd[:, i, 1:2], ALU.subtract,
                                        ALU.mult).then_inc(S["yo_ready"], 1)

        @block.tensor
        def _(pe):
            mm = nc.tensor.matmul
            pe.wait_ge(S["consts_made"], 1)
            pe.wait_ge(S["edges_f"], 1)
            for which in range(2):
                for k in range(CK):
                    ins = nc.tensor.transpose(bank(which)[0:PT, k * CHUNKS:(k + 1) * CHUNKS], e_f[:, which, k],
                                              ident[0:CHUNKS, 0:CHUNKS])
                ins.then_inc(S["edgesT_ps"], 1)
            pe.wait_ge(S["reach_sb"], 1)
            for w in range(2):
                ins = nc.tensor.transpose(bank(2)[0:NT, w * 128:w * 128 + CHUNKS], reach[:, 2 + w],
                                          ident[0:CHUNKS, 0:CHUNKS])
            ins.then_inc(S["reachT_ps"], 1)
            pe.wait_ge(S["ab_sb"], 1)
            mm(bank(3)[0:1, 0:NT], ab[:, 0:1], ident[0:NT, 0:NT], start=True, stop=True)
            mm(bank(3)[0:1, NT:2 * NT], ab[:, 1:2], ident[0:NT, 0:NT], start=True, stop=True)
            mm(bank(3)[0:1, 2 * NT:3 * NT], ab[:, 2:3], before[:], start=True, stop=False)
            mm(bank(3)[0:1, 2 * NT:3 * NT], ab[:, 0:1], ident[0:NT, 0:NT], start=False, stop=True).then_inc(S["rows_ps"], 1)
            pe.wait_ge(S["table_sb"], 1)
            pe.wait_ge(S["edgesT_sb"], 2)

            pe.sem_inc(S["onehot_free"], CK * AHEAD + CK)
            pe.sem_inc(S["acc_free"], 2)
            with pe.Fori(0, NT // 2) as b2:
                for half in range(2):
                    b = 2 * b2 + half
                    acc = ps[0:PT, half * 3 * BANK:half * 3 * BANK + N]
                    first, end, ahead = chunks_of(pe, b)
                    pe.wait_ge(S["acc_free"], b + 1)
                    for o, w in COLS:
                        mm(acc[:, o:o + w], ident16, diag[:, ds((N - PT) - b * PT + o, w)], start=True, stop=False,
                           skip_group_check=True)
                    with pe.Fori(first, end) as c:
                        g = ahead + c
                        pe.wait_ge(S["dst_ready"], g + 1 + DSLOTS)
                        for k in range(CK):
                            pe.wait_ge(S["onehot_ready"], CK * g + k + 1)
                            for o, w in COLS:
                                ins = mm(acc[:, o:o + w],
                                         dst1h[:, ds(g % 2, 1), k, 0:PT].rearrange("p o n -> p (o n)"),
                                         src1h[:, k, o:o + w], start=False, stop=False, skip_group_check=True)
                            ins.then_inc(S["onehot_free"], 1)
                    for o, w in COLS:
                        ins = mm(acc[:, o:o + 2], zero16, diag[:, 0:2], start=False, stop=True,
                                 skip_group_check=True)
                    ins.then_inc(S["acc_ready"], 1)

            pe.wait_ge(S["x_in"], 16)
            pe.wait_ge(S["acc_free"], 2 + NT)
            for i in range(KT * len(GROUPS)):
                k, (g, w) = i // len(GROUPS), GROUPS[i % len(GROUPS)]
                if i >= 4:
                    pe.wait_ge(S["xT_odd" if i % 2 else "xT_even"], (i - 4) // 2 + 1)
                for t in range(w):
                    ins = nc.tensor.transpose(bank(4 + i % 4)[:, t * PT:(t + 1) * PT],
                                              xin[:, g + t, k * KP:(k + 1) * KP], ident[0:PT, 0:PT])
                ins.then_inc(S["xT_ps"], 1)
            pe.wait_ge(S["wah_in"], 16)
            pe.wait_ge(S["xT_even"], KT * len(GROUPS) // 2)
            pe.wait_ge(S["xT_odd"], KT * len(GROUPS) // 2)
            for m in range(KT):
                if m >= 2:
                    pe.wait_ge(S["x1_sb"], m - 1)
                for k in range(KT):
                    for o, w in COLS:
                        oo = (m % 2) * 3 * BANK + o
                        ins = mm(ps[:, oo:oo + w], W_ah_sb[:, k, m * KP:(m + 1) * KP], xT[:, k, o:o + w],
                                 start=(k == 0), stop=(k == KT - 1))
                    if k == KT - 1:
                        ins.then_inc(S["x1_ps"], 1)
                    step = KT * m + k
                    if step < NT * len(GROUPS):
                        j, (g, w) = step // len(GROUPS), GROUPS[step % len(GROUPS)]
                        if step >= 2:
                            pe.wait_ge(S["cntT_sb"], step - 1)
                        for t in range(w):
                            ins = nc.tensor.transpose(bank(6 + step % 2)[0:PT, t * PT:(t + 1) * PT],
                                                      cnt[:, g + t, j * PT:(j + 1) * PT], ident[0:PT, 0:PT])
                        ins.then_inc(S["cntT_ps"], 1)
            pe.wait_ge(S["x1_sb"], KT)
            pe.wait_ge(S["v_made"], 2 * HEADS * KT * LAYERS)
            for k in range(KT):
                for o, w in COLS:
                    ins = mm(ps[0:2 * LH, o:o + w], V[:, k], x1T[:, k, o:o + w], start=(k == 0), stop=(k == KT - 1))
                ins.then_inc(S["x1_used"], 1)
            pe.wait_ge(S["cntT_sb"], NT * len(GROUPS))
            pe.wait_ge(S["asadT_sb"], 1)
            for t in range(NT):
                ins = nc.tensor.transpose(bank(7)[0:PT, t * 2 * LH:(t + 1) * 2 * LH], asadT[:, t * PT:(t + 1) * PT],
                                          ident[0:2 * LH, 0:2 * LH])
            ins.then_inc(S["asad_ps"], 1)
            pe.sem_inc(S["h_sb"], 4)
            pe.sem_inc(S["p_used"], PSLOTS)
            pe.wait_ge(S["x1_hi"], KT)
            pe.wait_ge(S["x1_lo"], KT)

            def h_part(l, c, last):
                pe.wait_ge(S["w_hi"], 2 * l + c + 1)
                pe.wait_ge(S["w_lo"], 2 * l + c + 1)
                for t in range(NT):
                    pe.wait_ge(S["h_sb"], NT * (2 * l + c) + t + 1)
                    for k in range(KT):
                        for n, (xx, ww) in enumerate(((x1_hi, Wl_hi), (x1_hi, Wl_lo), (x1_lo, Wl_hi))):
                            ins = mm(bank((2 * c + t) % 4)[0:PT, 0:HALF], xx[:, k, t * PT:(t + 1) * PT], ww[c][:, k],
                                     start=(k == 0 and n == 0), stop=(k == KT - 1 and n == 2))
                    ins.then_inc(S["h_ps"], 1)
                    if t == U_AT and last and c == 1:
                        shifts(1)

            def shifts(count):
                pe.wait_ge(S["amax_done"], count)
                for i, (g, w) in enumerate(GROUPS):
                    for tt in range(w):
                        ins = nc.tensor.transpose(bank(5 + i)[0:2 * LH, tt * PT:(tt + 1) * PT], u[:, g + tt],
                                                  ident[0:PT, 0:PT])
                    ins.then_inc(S["uT_ps"], 1)

            with pe.Fori(0, LAYERS - 1) as l:
                for c in range(2):
                    h_part(l, c, False)
            for c in range(2):
                h_part(LAYERS - 1, c, True)

            pe.wait_ge(S["uT_sb"], len(GROUPS))
            pe.wait_ge(S["h_sb"], 4 + PARTS * NT)
            pe.sem_inc(S["attT_ps"], 1)

            def tile(p, r):
                p, r = p + r // (2 * NT), r % (2 * NT)
                q, j = r // NT, r % NT
                if j == 0:
                    pe.wait_ge(hB_in[q], 16 * p + 16)
                pe.wait_ge(S["p_ready"], 2 * NT * p + r + 1)
                for t in OWN_FIRST:
                    if j == 0 and t == 4:
                        pe.wait_ge(S["out_evac"], NT * (2 * p + q) + 1)
                        if q == 1:
                            pe.wait_ge(S["attT_sb"], 9 * p + 1)
                    if j == 0 and t in (0, 2):
                        pe.wait_ge(S["out_evac"], NT * (2 * p + q) + t + 3)
                    o = out_at(q, t)
                    ins = mm(ps[0:PT, o:o + HW], prob[r % PSLOTS][:, t * PT:(t + 1) * PT], hB[:, q, j],
                             start=(j == 0 and t % 2 == 0), stop=(j == NT - 1), skip_group_check=True)
                ins.then_inc(S["p_used"], 1)

            def features(p, k):
                if k == 0:
                    pe.wait_ge(S["out_evac"], NT * (2 * p + 3) + 1)
                for i, (g, w) in enumerate(GROUPS):
                    if k > 0:
                        pe.wait_ge(S["attT_sb"], 9 * p + 3 * (k - 1) + i + 2)
                    else:
                        pe.wait_ge(S["attT_sb"], 9 * p + 1)
                    for t in range(w):
                        ins = nc.tensor.transpose(bank(5 + i)[:, t * PT:(t + 1) * PT],
                                                  att[:, g + t, k * KP:(k + 1) * KP], ident[0:PT, 0:PT])
                    ins.then_inc(S["attT_ps"], 1)

            def pair(p, last, shifts_here=False):
                for r in range(FEAT, 2 * NT if last else 2 * NT + FEAT):
                    if shifts_here and r == NT:
                        pe.wait_ge(S["uT_sb"], 2 * len(GROUPS))
                    tile(p, r)
                    if r >= 2 * NT + FEAT - PK:
                        features(p, r - (2 * NT + FEAT - PK))

            for r in range(FEAT):
                tile(0, r)
            with pe.Fori(0, PAIRS - 2) as p:
                pair(p, False)
            pe.wait_ge(S["attT_sb"], 9 * (PAIRS - 2) + 1)
            shifts(2)
            pair(PAIRS - 2, False, shifts_here=True)
            pair(PAIRS - 1, True)

            pe.wait_ge(S["wo_in"], 16)
            pe.wait_ge(S["first_in"], 16)
            pe.wait_ge(S["out_evac"], NT * LH + 1)
            for k in range(OK):
                if k == HEAD_START:
                    for kk in range(PK):
                        features(PAIRS - 1, kk)
                if k == early:
                    pe.wait_ge(S["attT_sb"], 9 * PAIRS + 1)
                for c in range(2):
                    o = (2 + c) * BANK
                    ins = mm(ps[0:PT, o:o + HALF], xs_first[:, k] if k < early else xsT[:, k - early, 0:PT], Wo_sb[:, k, c * HALF:(c + 1) * HALF],
                             start=(k == 0), stop=(k == OK - 1))
                ins.then_inc(S["wo_used"], 1)
            pe.wait_ge(S["wo_used"], OK)
            pe.sem_inc(S["y_ps"], 1)
            for t in range(1, NT):
                i = t % 2
                pe.wait_ge(S["xs_hi"], t)
                pe.wait_ge(S["xs_lo"], t)
                if t >= 2:
                    pe.wait_ge(S["y_sum"], t - 1)
                for k in range(OK):
                    if t == 1:
                        pe.wait_ge(S["wo_lo"], k + 1)
                        if k == early:
                            pe.wait_ge(S["late_hi"], 1)
                            pe.wait_ge(S["late_lo"], 1)
                    for c in range(2):
                        o = ((1 - i) * 2 + c) * BANK
                        half = slice(c * HALF, (c + 1) * HALF)
                        for n, (xx, ww) in enumerate(((xs_hi, Wo_hi), (xs_hi, Wo_lo), (xs_lo, Wo_hi))):
                            ins = mm(ps[0:PT, o:o + HALF], xx[i][:, k], ww[:, k, half],
                                     start=(k == 0 and n == 0), stop=(k == OK - 1 and n == 2))
                ins.then_inc(S["y_ps"], 1)


_OUT = (N, D)


def kernel(**inputs):
    import numpy as np
    import concourse.bacc as bacc
    from concourse.bass_utils import run_bass_kernel_spmd

    i = {k: np.asarray(v) for k, v in inputs.items()}
    p = "L0_gnn_"
    arrays = {
        "x": i["x"], "src": i["src"], "dst": i["dst"],
        "W_ah": i[p + "W_ah"],
        "b_ah": i[p + "b_ah"].reshape(KT, KP).T,
        "W_all": np.stack([i[f"{p}W{l}"] for l in range(LAYERS)]),
        "a_all": np.stack([np.stack([i[f"{p}a_src{l}"].reshape(D), i[f"{p}a_dst{l}"].reshape(D)])
                           for l in range(LAYERS)]),
        "b_all": np.stack([i[f"{p}b{l}"] for l in range(LAYERS)]).reshape(OK, KP).T,
        "W_out": i[p + "W_out"],
        "b_out": i[p + "b_out"].reshape(1, D),
    }
    arrays = {f"in_{k}": np.ascontiguousarray(v) for k, v in arrays.items()}
    nc = bacc.Bacc("TRN2", target_bir_lowering=False, num_devices=1)
    args = [nc.dram_tensor(k, v.shape, mybir.dt.from_np(v.dtype), kind="ExternalInput").ap()
            for k, v in arrays.items()]
    args.append(nc.dram_tensor("out_0", _OUT, mybir.dt.float32, kind="ExternalOutput").ap())
    gnn_program(nc, *args)
    r = run_bass_kernel_spmd(nc, [arrays], core_ids=[0])
    return r.results[0]["out_0"]
```
